# Optimizing a Trainium2 kernel written in Bass

```python
import numpy as np
import jax
import jax.numpy as jnp

def _softmax(x, axis=-1):
    return jax.nn.softmax(x, axis=axis)

def _gelu(x):
    return jax.nn.gelu(x, approximate=True)

def _silu(x):
    return jax.nn.silu(x)

def _sigmoid(x):
    return jax.nn.sigmoid(x)

def _layernorm(x, axis=-1, eps=1e-05):
    m = jnp.mean(x, axis=axis, keepdims=True)
    v = jnp.var(x, axis=axis, keepdims=True)
    return (x - m) / jnp.sqrt(v + eps)

def _scatter_add(tgt, idx, src, axis=0):
    return tgt.at[idx].add(src)

def _segment_sum(src, seg, n):
    return jax.ops.segment_sum(src, seg, n)
kernel_name = 'mk_conv_preact_d2_conv_nhwc128_r2_2c2d84'

def setup_inputs(seed: int=0):
    np.random.seed(seed)
    _w = jnp.asarray

    def _rec_inputs():
        import jax
        import jax.numpy as jnp
        _gk = jax.random.key(seed)
        x = -0.000125 + 0.9999 * jax.random.normal(jax.random.fold_in(_gk, 1), (1, 256, 256, 64), jnp.float32)
        return x
    x = _rec_inputs()

    def _L0_conv_setup():
        import jax, jax.numpy as jnp
        import numpy as np
        EPS = 1e-05

        def _ln(x, w, b):
            mu = jnp.mean(x, axis=-1, keepdims=True)
            var = jnp.var(x, axis=-1, keepdims=True)
            return (x - mu) * jax.lax.rsqrt(var + EPS) * w + b
        key = jax.random.key(seed)
        ks = jax.random.split(key, 10)
        B, N, C_Z, C_H = (1, 256, 64, 64)
        s = 0.02
        return {'z': jax.random.normal(ks[0], (B, N, N, C_Z), dtype=jnp.float32), 'mask': jnp.ones((B, N, N), dtype=jnp.float32), 'ln_in_w': jnp.ones((C_Z,), jnp.float32), 'ln_in_b': jnp.zeros((C_Z,), jnp.float32), 'w_ap': jax.random.normal(ks[1], (C_Z, C_H), jnp.float32) * s, 'b_ap': jnp.zeros((C_H,), jnp.float32), 'w_ag': jax.random.normal(ks[2], (C_Z, C_H), jnp.float32) * s, 'b_ag': jnp.ones((C_H,), jnp.float32), 'w_bp': jax.random.normal(ks[3], (C_Z, C_H), jnp.float32) * s, 'b_bp': jnp.zeros((C_H,), jnp.float32), 'w_bg': jax.random.normal(ks[4], (C_Z, C_H), jnp.float32) * s, 'b_bg': jnp.ones((C_H,), jnp.float32), 'w_g': jax.random.normal(ks[5], (C_Z, C_Z), jnp.float32) * s, 'b_g': jnp.ones((C_Z,), jnp.float32), 'w_z': jax.random.normal(ks[6], (C_H, C_Z), jnp.float32) * s, 'b_z': jnp.zeros((C_Z,), jnp.float32), 'ln_out_w': jnp.ones((C_H,), jnp.float32), 'ln_out_b': jnp.zeros((C_H,), jnp.float32)}
    _L0_conv_all = _L0_conv_setup()
    _L0_conv_in = {k: v for k, v in _L0_conv_all.items() if k in ('mask', 'ln_in_w', 'ln_in_b', 'w_ap', 'b_ap', 'w_ag', 'b_ag', 'w_bp', 'b_bp', 'w_bg', 'b_bg', 'w_g', 'b_g', 'w_z', 'b_z', 'ln_out_w', 'ln_out_b')}
    del _L0_conv_all

    def _L1_conv_setup():
        import jax, jax.numpy as jnp
        import numpy as np
        EPS = 1e-05
        AXIS = 1

        def _sparse_norm(x, alpha, beta):
            m = jnp.mean(x)
            v = jnp.var(x)
            nv = jax.lax.stop_gradient((x - m) * jax.lax.rsqrt(v + EPS))
            return alpha * nv + beta

        def _lin(x, W, b):
            return jnp.einsum('bijc,oc->bijo', x, W) + b
        key = jax.random.key(seed)
        ks = jax.random.split(key, 8)
        L, Cin, Cd = (256, 64, 64)
        g = 1.0 / np.sqrt(2.0)
        std_proj = g * np.sqrt(2.0 / (Cin + Cd))
        std_gate = np.sqrt(2.0 / (Cin + Cd))

        def w(k, o, i, s):
            return (jax.random.normal(k, (o, i), jnp.float32) * s).astype(jnp.float32)
        return {'z': jax.random.normal(ks[0], (1, L, L, Cin), jnp.float32), 'alpha_in': jnp.ones((1,), jnp.float32), 'beta_in': jnp.zeros((1,), jnp.float32), 'W_la': w(ks[1], Cd, Cin, std_proj), 'b_la': jnp.zeros((Cd,), jnp.float32), 'W_ga': w(ks[2], Cd, Cin, std_gate), 'b_ga': jnp.zeros((Cd,), jnp.float32), 'W_lb': w(ks[3], Cd, Cin, std_proj), 'b_lb': jnp.zeros((Cd,), jnp.float32), 'W_gb': w(ks[4], Cd, Cin, std_gate), 'b_gb': jnp.zeros((Cd,), jnp.float32), 'alpha_o': jnp.ones((1,), jnp.float32), 'beta_o': jnp.zeros((1,), jnp.float32), 'W_go': w(ks[5], Cin, Cin, std_gate), 'b_go': jnp.zeros((Cin,), jnp.float32), 'W_lo': w(ks[6], Cin, Cd, std_proj), 'b_lo': jnp.zeros((Cin,), jnp.float32)}
    _L1_conv_all = _L1_conv_setup()
    _L1_conv_in = {k: v for k, v in _L1_conv_all.items() if k in ('alpha_in', 'beta_in', 'W_la', 'b_la', 'W_ga', 'b_ga', 'W_lb', 'b_lb', 'W_gb', 'b_gb', 'alpha_o', 'beta_o', 'W_go', 'b_go', 'W_lo', 'b_lo')}
    del _L1_conv_all
    return {'x': x, 'L0_conv_mask': _L0_conv_in['mask'], 'L0_conv_ln_in_w': _L0_conv_in['ln_in_w'], 'L0_conv_ln_in_b': _L0_conv_in['ln_in_b'], 'L0_conv_w_ap': _L0_conv_in['w_ap'], 'L0_conv_b_ap': _L0_conv_in['b_ap'], 'L0_conv_w_ag': _L0_conv_in['w_ag'], 'L0_conv_b_ag': _L0_conv_in['b_ag'], 'L0_conv_w_bp': _L0_conv_in['w_bp'], 'L0_conv_b_bp': _L0_conv_in['b_bp'], 'L0_conv_w_bg': _L0_conv_in['w_bg'], 'L0_conv_b_bg': _L0_conv_in['b_bg'], 'L0_conv_w_g': _L0_conv_in['w_g'], 'L0_conv_b_g': _L0_conv_in['b_g'], 'L0_conv_w_z': _L0_conv_in['w_z'], 'L0_conv_b_z': _L0_conv_in['b_z'], 'L0_conv_ln_out_w': _L0_conv_in['ln_out_w'], 'L0_conv_ln_out_b': _L0_conv_in['ln_out_b'], 'L1_conv_alpha_in': _L1_conv_in['alpha_in'], 'L1_conv_beta_in': _L1_conv_in['beta_in'], 'L1_conv_W_la': _L1_conv_in['W_la'], 'L1_conv_b_la': _L1_conv_in['b_la'], 'L1_conv_W_ga': _L1_conv_in['W_ga'], 'L1_conv_b_ga': _L1_conv_in['b_ga'], 'L1_conv_W_lb': _L1_conv_in['W_lb'], 'L1_conv_b_lb': _L1_conv_in['b_lb'], 'L1_conv_W_gb': _L1_conv_in['W_gb'], 'L1_conv_b_gb': _L1_conv_in['b_gb'], 'L1_conv_alpha_o': _L1_conv_in['alpha_o'], 'L1_conv_beta_o': _L1_conv_in['beta_o'], 'L1_conv_W_go': _L1_conv_in['W_go'], 'L1_conv_b_go': _L1_conv_in['b_go'], 'L1_conv_W_lo': _L1_conv_in['W_lo'], 'L1_conv_b_lo': _L1_conv_in['b_lo']}

def reference(x, L0_conv_mask, L0_conv_ln_in_w, L0_conv_ln_in_b, L0_conv_w_ap, L0_conv_b_ap, L0_conv_w_ag, L0_conv_b_ag, L0_conv_w_bp, L0_conv_b_bp, L0_conv_w_bg, L0_conv_b_bg, L0_conv_w_g, L0_conv_b_g, L0_conv_w_z, L0_conv_b_z, L0_conv_ln_out_w, L0_conv_ln_out_b, L1_conv_alpha_in, L1_conv_beta_in, L1_conv_W_la, L1_conv_b_la, L1_conv_W_ga, L1_conv_b_ga, L1_conv_W_lb, L1_conv_b_lb, L1_conv_W_gb, L1_conv_b_gb, L1_conv_alpha_o, L1_conv_beta_o, L1_conv_W_go, L1_conv_b_go, L1_conv_W_lo, L1_conv_b_lo):
    import jax
    import jax.numpy as jnp

    def _L0_conv_ref(z, mask, ln_in_w, ln_in_b, w_ap, b_ap, w_ag, b_ag, w_bp, b_bp, w_bg, b_bg, w_g, b_g, w_z, b_z, ln_out_w, ln_out_b):
        import jax, jax.numpy as jnp
        import numpy as np
        EPS = 1e-05

        def _ln(x, w, b):
            mu = jnp.mean(x, axis=-1, keepdims=True)
            var = jnp.var(x, axis=-1, keepdims=True)
            return (x - mu) * jax.lax.rsqrt(var + EPS) * w + b
        m = mask[..., None]
        zn = _ln(z, ln_in_w, ln_in_b)
        a = m * jax.nn.sigmoid(zn @ w_ag + b_ag) * (zn @ w_ap + b_ap)
        b = m * jax.nn.sigmoid(zn @ w_bg + b_bg) * (zn @ w_bp + b_bp)
        p = jnp.einsum('bikc,bjkc->bijc', a, b)
        x = _ln(p, ln_out_w, ln_out_b) @ w_z + b_z
        g = jax.nn.sigmoid(zn @ w_g + b_g)
        return x * g

    def _L1_conv_ref(z, alpha_in, beta_in, W_la, b_la, W_ga, b_ga, W_lb, b_lb, W_gb, b_gb, alpha_o, beta_o, W_go, b_go, W_lo, b_lo):
        import jax, jax.numpy as jnp
        import numpy as np
        EPS = 1e-05
        AXIS = 1

        def _sparse_norm(x, alpha, beta):
            m = jnp.mean(x)
            v = jnp.var(x)
            nv = jax.lax.stop_gradient((x - m) * jax.lax.rsqrt(v + EPS))
            return alpha * nv + beta

        def _lin(x, W, b):
            return jnp.einsum('bijc,oc->bijo', x, W) + b
        zn = _sparse_norm(z, alpha_in, beta_in)
        a = jax.nn.sigmoid(_lin(zn, W_ga, b_ga)) * _lin(zn, W_la, b_la)
        b = jax.nn.sigmoid(_lin(zn, W_gb, b_gb)) * _lin(zn, W_lb, b_lb)
        if AXIS == 1:
            k = jnp.einsum('bitc,bjtc->bijc', a, b)
        else:
            k = jnp.einsum('btic,btjc->bijc', a, b)
        kn = _sparse_norm(k, alpha_o, beta_o)
        return jax.nn.sigmoid(_lin(zn, W_go, b_go)) * _lin(kn, W_lo, b_lo)

    def _gn(v, G=32, eps=1e-05):
        B_, H_, W_, C_ = v.shape
        g = v.reshape(B_, H_, W_, G, C_ // G)
        m = jnp.mean(g, axis=(1, 2, 4), keepdims=True)
        s = jnp.var(g, axis=(1, 2, 4), keepdims=True)
        return ((g - m) / jnp.sqrt(s + eps)).reshape(v.shape)

    def _ln_c(v, eps=1e-06):
        m = jnp.mean(v, axis=-1, keepdims=True)
        s = jnp.var(v, axis=-1, keepdims=True)
        return (v - m) / jnp.sqrt(s + eps)

    def _ln_t(v, eps=1e-05):
        m = jnp.mean(v, axis=-1, keepdims=True)
        s = jnp.var(v, axis=-1, keepdims=True)
        return (v - m) / jnp.sqrt(s + eps)

    def _to_tokens(v):
        B_, H_, W_, C_ = v.shape
        return v.reshape(B_, H_ * W_, C_)

    def _from_tokens(t, like):
        return t.reshape(like.shape)
    x = x + _L0_conv_ref(_gn(x), L0_conv_mask, L0_conv_ln_in_w, L0_conv_ln_in_b, L0_conv_w_ap, L0_conv_b_ap, L0_conv_w_ag, L0_conv_b_ag, L0_conv_w_bp, L0_conv_b_bp, L0_conv_w_bg, L0_conv_b_bg, L0_conv_w_g, L0_conv_b_g, L0_conv_w_z, L0_conv_b_z, L0_conv_ln_out_w, L0_conv_ln_out_b)
    x = x + _L1_conv_ref(_gn(x), L1_conv_alpha_in, L1_conv_beta_in, L1_conv_W_la, L1_conv_b_la, L1_conv_W_ga, L1_conv_b_ga, L1_conv_W_lb, L1_conv_b_lb, L1_conv_W_gb, L1_conv_b_gb, L1_conv_alpha_o, L1_conv_beta_o, L1_conv_W_go, L1_conv_b_go, L1_conv_W_lo, L1_conv_b_lo)
    return x

_drawn_inputs = setup_inputs


def setup_inputs(seed=0):
    import zlib

    import numpy as np

    out = dict(_drawn_inputs(seed))
    spreads = {'L0_conv_ln_in_w': (1.0, 0.6),
     'L0_conv_ln_in_b': (0.0, 0.1),
     'L0_conv_b_ap': (0.0, 0.1),
     'L0_conv_b_ag': (1.0, 0.6),
     'L0_conv_b_bp': (0.0, 0.1),
     'L0_conv_b_bg': (1.0, 0.6),
     'L0_conv_b_g': (1.0, 0.6),
     'L0_conv_b_z': (0.0, 0.1),
     'L0_conv_ln_out_w': (1.0, 0.2),
     'L0_conv_ln_out_b': (0.0, 0.461),
     'L1_conv_b_la': (0.0, 0.1),
     'L1_conv_b_ga': (0.0, 0.671),
     'L1_conv_b_lb': (0.0, 0.1),
     'L1_conv_b_gb': (0.0, 0.54),
     'L1_conv_b_go': (0.0, 0.436),
     'L1_conv_b_lo': (0.0, 0.1)}
    factors = {'L0_conv_w_ag': 29.796, 'L0_conv_w_bg': 26.196, 'L0_conv_w_g': 8.0}
    for name, (base, spread) in spreads.items():
        noise = np.random.default_rng([zlib.crc32(name.encode()), seed]).standard_normal(out[name].shape)
        drawn = base * np.exp(spread * noise) if base else spread * noise
        out[name] = jnp.asarray(drawn.astype(out[name].dtype))
    for name, factor in factors.items():
        out[name] = (out[name] * factor).astype(out[name].dtype)
    return out
```

```python
import numpy as np
from contextlib import ExitStack

import concourse.bass as bass
from concourse import mybir

ROWS = 256
COLS = 256
CH = 64
P = 128
ROW = 2 * CH
GR = 4
NG = ROWS // GR
BANK = 512
CHUNK = 16
NQ = CH // CHUNK
LOAD_ROWS = 16
LOAD_SLOTS = 4
LG = LOAD_ROWS // GR
BR = 32
BG = BR // GR
NB = ROWS // BR
TG = 16
NT = NG // TG
QW = 4 * 2 * CHUNK
W_G = NQ * QW
W_Z = W_G + ROW
W_N = W_Z + ROW
EPS = 1e-5
SEL = 32 * 2 + 2 + 2 * (TG - 1) + 30

C_ID, C_GM, C_ONES, C_E0, C_NE0, C_N = 0, 128, 256, 384, 385, 386
L_CM, L_DROP, L_SEL, L_ECOL, L_BSEL, L_N = 0, 128, 256, 384, 512, 640
V_LNW, V_LNB, V_OW, V_OB, V_AI, V_BI, V_AO, V_BO, V_N = range(9)


def build(nc, x, mask, w0, w1, bias0, bias1, vecs, consts, norm_consts, spread, ones3, out):
    f32 = mybir.dt.float32
    bf16 = mybir.dt.bfloat16
    ALU = mybir.AluOpType
    ACT = mybir.ActivationFunctionType
    ds = bass.ds

    x_tok = x[0].rearrange("r (p q) c -> p r (q c)", q=2)
    out_tok = out[0].rearrange("r (p q) c -> p r (q c)", q=2)
    p_dram = nc.dram_tensor("p_scratch", [P, CH // 2, 2 * ROWS * 2], f32, kind="Internal").ap()
    p_blocks = p_dram.rearrange("p c (q r e) -> p (c q) (r e)", q=2, e=2)
    x1_dram = nc.dram_tensor("x1_scratch", [P, ROWS, ROW], f32, kind="Internal").ap()

    ctx = ExitStack()
    with ctx:
        def sb(name, cols, dt=f32):
            return ctx.enter_context(nc.sbuf_tensor(name, [P, cols], dt))

        def sem(name):
            return ctx.enter_context(nc.semaphore(name))

        XT = ctx.enter_context(nc.sbuf_tensor("XT", [P, ROWS, P], f32))
        AB = sb("AB", 2 * 2 * CHUNK * ROWS)
        CF = sb("CF", C_N)
        RAW = sb("RAW", W_N)
        EFF = sb("EFF", W_N)
        BROW = sb("BROW", W_N, bf16)
        ONES3 = sb("ONES3", P, bf16)
        MS = sb("MS", 2 * BANK)
        S1 = sb("S1", BANK)
        WK = sb("WK", 7 * BANK)
        REC = sb("REC", 6 * NG)
        VEC = sb("VEC", V_N)
        T = sb("T", 24)
        PS = ctx.enter_context(nc.psum_tensor("PS", [P, 8, BANK], f32))

        ident = CF[:, C_ID:C_ID + P]
        group_mean = CF[:, C_GM:C_GM + P]
        ones = CF[:, C_ONES:C_ONES + P]

        p_shift_all = EFF[:, 0:P]
        shift_all = EFF[:, W_Z:W_N]

        xs = AB[:, 0:LOAD_SLOTS * LOAD_ROWS * ROW].rearrange("p (s r m) -> p s r m", s=LOAD_SLOTS, m=ROW)
        at = LOAD_SLOTS * LOAD_ROWS * ROW

        def part(n):
            nonlocal at
            at += n
            return AB[:, at - n:at]

        NCF = part(L_N)
        maskn = part(2 * COLS)
        brow0 = part(W_N)
        spread_sb = part(TG * P // 2).bitcast(bf16)
        sq = part(2 * BANK).rearrange("p (s n) -> p s n", s=2)
        ve, sd, rt, tmp = (part(BANK) for _ in range(4))
        parts3 = part(BANK // 2).bitcast(bf16)
        cs = part(P)
        wW = part(W_N)
        lnb_col = part(P)
        lnb_all = part(P)
        assert at <= 2 * 2 * CHUNK * ROWS
        ab = AB[:, :].rearrange("p (q k r) -> p q k r", q=2, r=ROWS)
        ptb = AB[:, 0:2 * CH * BR * 2].rearrange("p (s m n) -> p s m n", s=2, n=2 * BR)
        xb = AB[:, 2 * CH * BR * 2:4 * CH * BR * 2].rearrange("p (s r m) -> p s r m", s=2, m=ROW)

        sig = WK[:, 0:4 * 256].rearrange("p (s t k) -> p s t k", s=4, k=2 * CHUNK)
        st = WK[:, 1024:1024 + 4 * BANK].rearrange("p (s n e) -> p s n e", s=2, e=2)
        sqp = WK[:, 6 * BANK:7 * BANK]
        pn = WK[:, 0:2 * BANK].rearrange("p (s r m) -> p s r m", s=2, m=ROW)
        pt = WK[:, 2 * BANK:4 * BANK].rearrange("p (s n) -> p s n", s=2)
        sg = [WK[:, 4 * BANK:5 * BANK], WK[:, 5 * BANK:6 * BANK], MS[:, 0:BANK], MS[:, BANK:2 * BANK]]
        maskT = MS[:, 0:BANK].rearrange("p (q r) -> p q r", q=2)
        S2 = MS[:, BANK:2 * BANK]
        brow1 = MS[:, 0:W_N]
        rstd2 = S1[:, :].rearrange("p (q r) -> p q r", q=2)

        consts_in = sem("consts_in")
        raw1_in = sem("raw1_in")
        brow1_in = sem("brow1_in")
        xs_in = [sem(f"xs_in{s}") for s in range(LOAD_SLOTS)]
        tr_done = sem("tr_done")
        xt_ready = sem("xt_ready")
        bn_done = sem("bn_done")
        mask_tr = sem("mask_tr")
        mask_ready = sem("mask_ready")
        dve_step = sem("dve_step")
        dve_chain = sem("dve_chain")
        s1_done = sem("s1_done")
        small_in = sem("small_in")
        small_out = sem("small_out")
        var_ready = sem("var_ready")
        std_ready = sem("std_ready")
        norm_ready = sem("norm_ready")
        weights_ready = sem("weights_ready")
        mm1_done = sem("mm1_done")
        zc_done = sem("zc_done")
        sq_ready = sem("sq_ready")
        mm2_done = sem("mm2_done")
        rb_zero = sem("rb_zero")
        rb_ready = sem("rb_ready")
        bc_done = sem("bc_done")
        zn_done = sem("zn_done")
        proj_done = sem("proj_done")
        sig_done = sem("sig_done")
        msk_done = sem("msk_done")
        prod_done = sem("prod_done")
        ein_done = sem("ein_done")
        st_ready = sem("st_ready")
        sqp_ready = sem("sqp_ready")
        acc_done = sem("acc_done")
        p_stored = [sem(f"p_stored{s}") for s in range(2)]
        p_in = [sem(f"p_in{s}") for s in range(2)]
        xb_in = [sem(f"xb_in{s}") for s in range(2)]
        xb_stored = [sem(f"xb_stored{s}") for s in range(2)]
        pn_done = sem("pn_done")
        tb_done = sem("tb_done")
        pt_ready = sem("pt_ready")
        g_done = sem("g_done")
        sg_done = sem("sg_done")
        z_done = sem("z_done")
        y_done = sem("y_done")
        xadd_done = sem("xadd_done")
        x1tr_done = sem("x1tr_done")
        x1t_ready = sem("x1t_ready")

        block = ctx.enter_context(nc.Block())

        def rounds(eng, body, n, peeled):
            for i in range(peeled):
                body(i)
            with eng.Fori(peeled, n) as i:
                body(i)

        def reached(eng, semaphore, value):
            if not isinstance(value, int) or value > 0:
                eng.wait_ge(semaphore, value)

        @block.sync
        def _(sp):
            def load_x(row, s):
                for h in range(2):
                    sp.dma_start(xs[:, s, h * LOAD_ROWS // 2:(h + 1) * LOAD_ROWS // 2, :],
                                 x_tok[:, ds(row + h * LOAD_ROWS // 2, LOAD_ROWS // 2), :]).then_inc(xs_in[s], 16)

            load_x(0 * LOAD_ROWS, 0)
            load_x(1 * LOAD_ROWS, 1)
            for dst, src in ((CF[:, :], consts), (NCF, norm_consts), (RAW[:, :], w0),
                             (brow0[0:2, :], bias0), (VEC[:, :], vecs), (spread_sb, spread), (ONES3[:, :], ones3),
                             (maskn.rearrange("p (h c) -> p h c", h=2),
                              mask[0].rearrange("(h p) c -> p h c", h=2))):
                sp.dma_start(dst, src).then_inc(consts_in, 16)
            load_x(2 * LOAD_ROWS, 2)
            load_x(3 * LOAD_ROWS, 3)
            with sp.Fori(1, ROWS // LOAD_ROWS // LOAD_SLOTS) as t4:
                for s in range(LOAD_SLOTS):
                    row = sp.snap(t4 * (LOAD_SLOTS * LOAD_ROWS) + s * LOAD_ROWS)
                    sp.wait_ge(tr_done, t4 * (LG * LOAD_SLOTS) + LG * (s + 1 - LOAD_SLOTS))
                    load_x(row, s)
            for layer in range(2):
                if layer == 0:
                    sp.wait_ge(small_out, 3)
                    sp.dma_start(RAW[:, :], w1).then_inc(raw1_in, 16)
                with sp.Fori(0, NQ) as q:
                    for pair in range(CHUNK // 2):
                        at_pair = sp.snap(q * (CHUNK // 2) + pair)
                        sp.wait_ge(st_ready, q * CHUNK + (2 * pair + 2 + CH * layer))
                        sp.dma_start(p_dram[:, ds(at_pair, 1), :],
                                     st[:, pair % 2].rearrange("p n e -> p (n e)").unsqueeze(1)
                                     ).then_inc(p_stored[pair % 2], 16)
                for s in range(2):
                    sp.wait_ge(p_stored[s], 16 * (CH // 4) * (layer + 1))
                sp.wait_ge(ein_done, CH * (layer + 1))
                sp.wait_ge(acc_done, CH * (layer + 1))

                source, sink = (x_tok, x1_dram) if layer == 0 else (x1_dram, out_tok)

                def load_block(row, s):
                    for h in range(4):
                        sp.dma_start(ptb[:, s, h * CH // 4:(h + 1) * CH // 4, :],
                                     p_blocks[:, h * CH // 4:(h + 1) * CH // 4, ds(row * 2, 2 * BR)]
                                     ).then_inc(p_in[s], 16)
                    for h in range(4):
                        sp.dma_start(xb[:, s, h * BR // 4:(h + 1) * BR // 4, :],
                                     source[:, ds(row + h * BR // 4, BR // 4), :]).then_inc(xb_in[s], 16)

                def store_block(row, s):
                    sp.dma_start(sink[:, ds(row, BR), :], xb[:, s]).then_inc(xb_stored[s], 16)

                load_block(0, 0)
                load_block(BR, 1)
                with sp.Fori(0, NB // 2 - 1) as b2:
                    for s in range(2):
                        row = sp.snap(b2 * (2 * BR) + s * BR)
                        after = sp.snap(b2 * (2 * BR) + (s + 2) * BR)
                        groups = sp.snap(b2 * (2 * BG) + ((s + 1) * BG + NG * layer))
                        stores = sp.snap(b2 * 16 + 16 * (1 + NB // 2 * layer))
                        sp.wait_ge(xadd_done, groups)
                        store_block(row, s)
                        sp.wait_ge(xb_stored[s], stores)
                        sp.wait_ge(tb_done, groups)
                        if layer == 0:
                            sp.wait_ge(x1tr_done, groups)
                        load_block(after, s)
                for s in range(2):
                    sp.wait_ge(xadd_done, NG - (1 - s) * BG + NG * layer)
                    store_block((NB - 2 + s) * BR, s)
                for s in range(2):
                    sp.wait_ge(xb_stored[s], 16 * (NB // 2) * (layer + 1))
                if layer == 0:
                    sp.wait_ge(xadd_done, NG)
                    sp.dma_start(brow1[0:2, :], bias1).then_inc(brow1_in, 16)

        @block.tensor
        def _(pe):
            def mm(dst, lhsT, rhs, start=True, stop=True):
                return nc.tensor.matmul(dst, lhsT, rhs, start=start, stop=stop)

            N_CONSTS = 8
            pe.wait_ge(consts_in, 16 * N_CONSTS)

            def transpose_loads(t4):
                for s in range(LOAD_SLOTS):
                    for u in range(LG):
                        g = s * LG + u
                        if u == 0:
                            pe.wait_ge(xs_in[s], t4 * 32 + 32)
                        reached(pe, xt_ready, t4 * (LG * LOAD_SLOTS) + (g - 3))
                        for r in range(GR):
                            last = nc.tensor.transpose(PS[:, g % 4, r * P:(r + 1) * P], xs[:, s, u * GR + r, :], ident)
                        last.then_inc(tr_done, 1)

            transpose_loads(0)
            for q in range(2):
                for h in range(2):
                    src = maskn.rearrange("p (h c q) -> p h q c", h=2, q=2)[:, h, q]
                    last = nc.tensor.transpose(PS[:, 7, (2 * q + h) * P:(2 * q + h + 1) * P], src, ident)
            last.then_inc(mask_tr, 1)
            with pe.Fori(1, ROWS // LOAD_ROWS // LOAD_SLOTS) as t4:
                transpose_loads(t4)

            smalls = [0]

            def small(pairs):
                smalls[0] += 1
                pe.wait_ge(small_in, smalls[0])
                for args in pairs:
                    last = mm(*args)
                last.then_inc(small_out, 1)

            pe.wait_ge(mask_ready, 1)
            small([(PS[:, 7, 0:1], group_mean, T[:, 0:1])])
            small([(PS[:, 7, 2:3], group_mean, T[:, 3:4])])
            cm, drop = NCF[:, L_CM:L_CM + P], NCF[:, L_DROP:L_DROP + P]
            bsel = NCF[0:2, L_BSEL:L_BSEL + P]
            small([(PS[:, 7, 4:5], cm, T[:, 8:9]),
                   (PS[:, 5, :], drop, wW[:, 0:BANK], True, False),
                   (PS[:, 5, :], lnb_col, RAW[:, 0:BANK], False, False),
                   (PS[:, 5, :], bsel, brow0[0:2, 0:BANK], False, True),
                   (PS[:, 6, 0:P], drop, wW[:, W_G:W_Z], True, False),
                   (PS[:, 6, 0:P], lnb_col, RAW[:, W_G:W_Z], False, False),
                   (PS[:, 6, 0:P], bsel, brow0[0:2, W_G:W_Z], False, True),
                   (PS[:, 6, P:2 * P], cm, wW[:, W_Z:W_N]),
                   (PS[:, 6, 2 * P:3 * P], lnb_all, RAW[:, W_Z:W_N], True, False),
                   (PS[:, 6, 2 * P:3 * P], ones[0:2, :], brow0[0:2, W_Z:W_N], False, True)])
            pe.wait_ge(norm_ready, 1)

            def centre(t):
                for u in range(TG + 1):
                    if u < TG:
                        reached(pe, sq_ready, t * TG + (u - 3))
                        mm(PS[:, u % 4, :], cs, XT[:, ds(t * (TG * GR) + u * GR, GR), :].rearrange("p r n -> p (r n)")
                           ).then_inc(mm1_done, 1)
                    if u >= 1:
                        v = u - 1
                        pe.wait_ge(sq_ready, t * TG + (v + 1))
                        if v == 0:
                            reached(pe, var_ready, t + 1)
                        s0 = L_SEL + 30 - 2 * v
                        mm(PS[0:96, 4, :], NCF[:, s0:s0 + 96], sq[:, v % 2], v == 0, v == TG - 1).then_inc(mm2_done, 1)

            def spread_rstd(t):
                pe.wait_ge(rb_ready, t + 1)
                for u in range(TG):
                    reached(pe, zn_done, t * TG + max(u - 1, 0))
                    mm(PS[:, 5 + u % 2, :], spread_sb[:, u * P:(u + 1) * P], parts3).then_inc(bc_done, 1)

            def round_(t):
                centre(t)
                if not isinstance(t, int) or t > 0:
                    spread_rstd(t - 1)

            rounds(pe, round_, NT, 2)
            spread_rstd(NT - 1)
            pe.wait_ge(zn_done, NG)

            for layer in range(2):
                free = sqp_ready if layer == 0 else st_ready

                def chunk(q):
                    for g in range(NG):
                        bank = PS[:, g % 4, :]
                        if g >= 4:
                            pe.wait_ge(prod_done, q * NG + (g - 3 + NQ * NG * layer))
                        if layer == 1:
                            mm(bank, ONES3[:, :], BROW[:, ds(q * QW, QW)].unsqueeze(1).to_broadcast([P, GR, QW]), True, False)
                        for r in range(GR):
                            last = mm(bank[:, r * QW:(r + 1) * QW], XT[:, g * GR + r, :], EFF[:, ds(q * QW, QW)],
                                      layer == 0, layer == 0 or r == GR - 1)
                        last.then_inc(proj_done, 1)
                    pe.wait_ge(prod_done, q * NG + (NG + NQ * NG * layer))
                    for c in range(CHUNK):
                        reached(pe, free, q * CHUNK + (max(c - 3, 0) + CH * layer))
                        for jq in range(2):
                            for kq in range(2):
                                last = mm(PS[:, 4 + c % 4, jq * ROWS:(jq + 1) * ROWS],
                                          ab[:, kq, CHUNK + c, jq::2], ab[:, kq, c, :], kq == 0, kq == 1)
                        last.then_inc(ein_done, 1)

                rounds(pe, chunk, NQ, 1 - layer)

                if layer == 1:
                    small([(PS[:, 7, 0:1], ones, T[:, 0:1])])
                    small([(PS[:, 7, 2:3], ones, T[:, 3:4])])
                    small([(PS[:, 6, 0:P], p_shift_all, RAW[:, W_Z:W_N], True, False),
                           (PS[:, 6, 0:P], ones[0:2, :], brow1[0:2, W_Z:W_N], False, True)])
                pe.wait_ge(weights_ready, layer + 1)
                base = NG * layer
                pe.wait_ge(free, CH * (layer + 1) if layer == 1 else CH)
                for step in range(NG + 3):
                    g = step
                    if g < NG:
                        pe.wait_ge(pn_done, base + g + 1)
                        reached(pe, pt_ready, base + g - 1)
                        for r in range(GR):
                            last = nc.tensor.transpose(PS[:, g % 2, r * P:(r + 1) * P], pn[:, g % 2, r, :], ident)
                        last.then_inc(tb_done, 1)
                        bank = PS[:, 4 + g % 2, :]
                        reached(pe, sg_done, base + g - 1)
                        if layer == 1:
                            mm(bank, ONES3[:, :], BROW[:, W_G:W_Z].unsqueeze(1).to_broadcast([P, GR, ROW]), True, False)
                        for r in range(GR):
                            last = mm(bank[:, r * P:(r + 1) * P], XT[:, g * GR + r, :], EFF[:, W_G:W_Z],
                                      layer == 0, layer == 0 or r == GR - 1)
                        last.then_inc(g_done, 1)
                    g = step - 1
                    if 0 <= g < NG:
                        pe.wait_ge(pt_ready, base + g + 1)
                        reached(pe, y_done, base + g - 1)
                        bank = PS[:, 2 + g % 2, :]
                        mm(bank, ONES3[:, :], BROW[:, W_Z:W_N].unsqueeze(1).to_broadcast([P, GR, ROW]), True, False)
                        for r in range(GR):
                            last = mm(bank[:, r * P:(r + 1) * P], pt[:, g % 2, r * P:(r + 1) * P], EFF[:, W_Z:W_N],
                                      False, r == GR - 1)
                        last.then_inc(z_done, 1)
                    g = step - 3
                    if layer == 0 and 0 <= g < NG:
                        pe.wait_ge(xadd_done, g + 1)
                        reached(pe, x1t_ready, g - 1)
                        for r in range(GR):
                            last = nc.tensor.transpose(PS[:, 6 + g % 2, r * P:(r + 1) * P],
                                                       xb[:, (g // BG) % 2, (g % BG) * GR + r, :], ident)
                        last.then_inc(x1tr_done, 1)

                if layer == 0:
                    pe.wait_ge(x1t_ready, NG)
                    small([(PS[:, 7, 0:1], group_mean, T[:, 0:1])])
                    small([(PS[:, 7, 2:3], group_mean, T[:, 3:4])])
                    small([(PS[:, 7, 4:5], ones, T[:, 10:11])])
                    small([(PS[:, 7, 6:7], ones, T[:, 12:13])])
                    pe.wait_ge(brow1_in, 16)
                    small([(PS[:, 5, :], shift_all, RAW[:, 0:BANK], True, False),
                           (PS[:, 5, :], ones[0:2, :], brow1[0:2, 0:BANK], False, True),
                           (PS[:, 6, 0:P], shift_all, RAW[:, W_G:W_Z], True, False),
                           (PS[:, 6, 0:P], ones[0:2, :], brow1[0:2, W_G:W_Z], False, True)])
                    pe.wait_ge(norm_ready, 2)

        @block.scalar
        def _(act):
            def transposed(t4):
                for g in range(LG * LOAD_SLOTS):
                    n = t4 * (LG * LOAD_SLOTS) + g
                    act.wait_ge(tr_done, n + 1)
                    nc.scalar.activation(XT[:, ds(n * GR, GR), :].rearrange("p r n -> p (r n)"), PS[:, g % 4, :],
                                         ACT.Copy).then_inc(xt_ready, 1)

            transposed(0)
            act.wait_ge(mask_tr, 1)
            nc.scalar.activation(maskT.rearrange("p q r -> p (q r)"), PS[:, 7, :], ACT.Copy).then_inc(mask_ready, 1)
            with act.Fori(1, ROWS // LOAD_ROWS // LOAD_SLOTS) as t4:
                transposed(t4)

            def root(n, dst, src):
                act.wait_ge(var_ready, n)
                nc.scalar.activation(dst, src, ACT.Sqrt).then_inc(std_ready, 1)

            root(1, T[:, 5:6], T[:, 4:5])
            act.wait_ge(norm_ready, 1)

            def centred(t):
                for u in range(TG):
                    n = t * TG + u
                    act.wait_ge(mm1_done, n + 1)
                    nc.scalar.activation(XT[:, ds(n * GR, GR), :].rearrange("p r n -> p (r n)"), PS[:, u % 4, :],
                                         ACT.Identity, bias=T[:, 15:16], scale=CF[:, C_NE0:C_NE0 + 1]
                                         ).then_inc(zc_done, 1)
                    reached(act, mm2_done, n - 1)
                    nc.scalar.activation(sq[:, u % 2], PS[:, u % 4, :], ACT.Square, bias=T[:, 14:15]
                                         ).then_inc(sq_ready, 1)
                root(t + 2, sd[0:96, :], ve[0:96, :])

            centred(0)
            with act.Fori(1, NT) as t:
                centred(t)

            for layer in range(2):
                base = NQ * NG * layer

                def gates(q, g4):
                    for u in range(4):
                        n = q * NG + (g4 * 4 + (base + u))
                        act.wait_ge(proj_done, n + 1)
                        reached(act, prod_done, q * NG + base if isinstance(g4, int) else n - 3)
                        nc.scalar.activation(
                            sig[:, u], PS[:, u, :].rearrange("p (t k) -> p t k", k=4 * CHUNK)[:, :, 0:2 * CHUNK],
                            ACT.Sigmoid).then_inc(sig_done, 1)

                def chunk(q):
                    gates(q, 0)
                    with act.Fori(1, NG // 4) as g4:
                        gates(q, g4)
                    for c in range(CHUNK):
                        s = (c // 2) % 2
                        act.wait_ge(ein_done, q * CHUNK + (c + 1 + CH * layer))
                        if c % 2 == 0:
                            reached(act, p_stored[s], q * (16 * CHUNK // 4) + 16 * (c // 4 + CH // 4 * layer))
                            reached(act, acc_done, q * CHUNK + (max(c - 2, 0) + CH * layer))
                        nc.scalar.activation(st[:, s, :, c % 2], PS[:, 4 + c % 4, :], ACT.Copy).then_inc(st_ready, 1)
                        if layer == 0:
                            reached(act, acc_done, q * CHUNK + c)
                            nc.scalar.activation(sqp, PS[:, 4 + c % 4, :], ACT.Square).then_inc(sqp_ready, 1)

                rounds(act, chunk, NQ, 1 - layer)

                base = NG * layer
                if layer == 0:
                    root(NT + 2, WK[:, BANK:2 * BANK], WK[:, 0:BANK])
                else:
                    root(NT + 5, T[:, 5:6], T[:, 4:5])

                def finish_steps(g0, n_steps, lo):
                    for k in range(n_steps):
                        g = g0 + k
                        if lo[0] <= k < lo[1]:
                            act.wait_ge(tb_done, g + (1 + base))
                            reached(act, z_done, g + (base - 1))
                            nc.scalar.activation(pt[:, k % 2], PS[:, k % 2, :], ACT.Copy).then_inc(pt_ready, 1)
                            act.wait_ge(g_done, g + (1 + base))
                            reached(act, xadd_done, g + (base - 3))
                            nc.scalar.activation(sg[k % 4], PS[:, 4 + k % 2, :], ACT.Sigmoid).then_inc(sg_done, 1)
                        if layer == 0 and lo[2] <= k < lo[3]:
                            h = g - 4
                            act.wait_ge(x1tr_done, h + 1)
                            nc.scalar.activation(XT[:, ds(h * GR, GR), :].rearrange("p r n -> p (r n)"),
                                                 PS[:, 6 + k % 2, :], ACT.Copy).then_inc(x1t_ready, 1)

                finish_steps(0, 16, (0, 16, 4, 16))
                with act.Fori(1, NG // 16) as i:
                    finish_steps(i * 16, 16, (0, 16, 0, 16))
                finish_steps(NG, 4, (0, 0, 0, 4))
                if layer == 0:
                    root(NT + 3, T[:, 5:6], T[:, 4:5])
                    root(NT + 4, T[:, 17:18], T[:, 16:17])

        @block.gpsimd
        def _(pool):
            pool.wait_ge(mask_ready, 1)

            with pool.Fori(0, NQ) as q:
                with pool.Fori(0, NG // 4) as g4:
                    for u in range(4):
                        pool.wait_ge(sig_done, q * NG + (g4 * 4 + (u + 1)))
                        rows = maskT[:, :, ds(g4 * (4 * GR) + u * GR, GR)].rearrange("p q r -> p r q")
                        tile = sig[:, u].rearrange("p (r q) k -> p r q k", q=2)
                        nc.gpsimd.tensor_tensor(tile, tile, rows.unsqueeze(3).to_broadcast([P, GR, 2, 2 * CHUNK]),
                                                ALU.mult).then_inc(msk_done, 1)
            for layer in range(2):
                base = NG * layer
                with pool.Fori(0, NB // 2) as b2:
                    for s in range(2):
                        pool.wait_ge(xb_in[s], b2 * 64 + 64 * (1 + NB // 2 * layer))
                        for u in range(BG):
                            g = s * BG + u
                            pool.wait_ge(y_done, b2 * (2 * BG) + (g + 1 + base))
                            rows = xb[:, s, u * GR:(u + 1) * GR, :].rearrange("p r m -> p (r m)")
                            nc.gpsimd.tensor_tensor(rows, rows, sg[g % 4], ALU.add).then_inc(xadd_done, 1)

        @block.vector
        def _(dve):
            steps = [0]
            counts = {"small": 0}

            def step(ins):
                steps[0] += 1
                ins.then_inc(dve_step, 1)
                dve.wait_ge(dve_step, steps[0])

            def answer():
                counts["small"] += 1
                dve.wait_ge(small_out, counts["small"])

            def col(i):
                return T[:, i:i + 1]

            V = nc.vector

            def final(ins, semaphore, value):
                ins.then_inc(semaphore, 1)
                dve.wait_ge(semaphore, value)

            def rsqrt(dst, var, std, n, tmp_):
                dve.wait_ge(std_ready, n)
                step(V.reciprocal(dst, std))
                step(V.tensor_tensor(tmp_, dst, dst, ALU.mult))
                step(V.tensor_tensor(tmp_, tmp_, var, ALU.mult))
                step(V.tensor_scalar(tmp_, tmp_, -0.5, 1.5, ALU.mult, ALU.add))
                return V.tensor_tensor(dst, dst, tmp_, ALU.mult)

            def group_norm(n):
                V.bn_aggr(T[:, 0:2], REC[:, :]).then_inc(small_in, 1)
                answer()
                step(V.tensor_copy(col(2), PS[:, 7, 0:1]))
                step(V.tensor_tensor(col(7), col(0), col(2), ALU.subtract))
                V.scalar_tensor_tensor(col(3), col(7), col(7), col(1), ALU.mult, ALU.add).then_inc(small_in, 1)
                answer()
                V.tensor_scalar(col(4), PS[:, 7, 2:3], EPS, None, ALU.add).then_inc(var_ready, 1)
                step(rsqrt(col(6), col(4), col(5), n, col(7)))
                step(V.scalar_tensor_tensor(col(8), col(2), -1.0, col(6), ALU.mult, ALU.mult))

            def split3(dst, src, n, w, done=step):
                left = WK[:, 0:n]
                step(V.tensor_copy(dst[0:1, :], src[0:1, :]))
                step(V.tensor_copy(w[:, 0:n], src))
                step(V.tensor_tensor(left, src, w[:, 0:n], ALU.subtract))
                step(V.tensor_copy(dst[32:33, :], left[32:33, :]))
                step(V.tensor_copy(w[:, 0:n], left))
                step(V.tensor_tensor(left, left, w[:, 0:n], ALU.subtract))
                done(V.tensor_copy(dst[64:65, :], left[64:65, :]))

            wk_bf = WK[:, 2 * BANK:3 * BANK].bitcast(bf16)
            step(V.memset(BROW[:, :], 0.0))
            step(V.memset(S1[:, :], 0.0))
            step(V.memset(S2, 0.0))
            step(V.memset(parts3[96:P, :], 1.0))

            def record(t4):
                for g in range(LG * LOAD_SLOTS):
                    n = t4 * (LG * LOAD_SLOTS) + g
                    dve.wait_ge(xt_ready, n + 1)
                    V.bn_stats(REC[:, ds(n * 6, 6)], XT[:, ds(n * GR, GR), :].rearrange("p r n -> p (r n)")
                               ).then_inc(bn_done, 1)

            with dve.Fori(0, ROWS // LOAD_ROWS // LOAD_SLOTS) as t4:
                record(t4)
            dve.wait_ge(bn_done, NG)
            group_norm(1)
            step(V.tensor_scalar(cs, NCF[:, L_CM:L_CM + P], col(6), None, ALU.mult))
            step(V.tensor_scalar(wW[:, 0:W_Z], RAW[:, 0:W_Z], VEC[:, V_LNW:V_LNW + 1], None, ALU.mult))
            step(V.tensor_scalar(wW[:, W_Z:W_N], RAW[:, W_Z:W_N], VEC[:, V_OW:V_OW + 1], None, ALU.mult))
            step(V.tensor_scalar(lnb_col, NCF[:, L_ECOL:L_ECOL + P], VEC[:, V_LNB:V_LNB + 1], None, ALU.mult))
            V.tensor_scalar(lnb_all, ones, VEC[:, V_OB:V_OB + 1], None, ALU.mult).then_inc(small_in, 1)
            answer()
            step(V.tensor_copy(col(14), PS[:, 7, 4:5]))
            step(V.scalar_tensor_tensor(col(15), col(14), CF[:, C_NE0:C_NE0 + 1], CF[:, C_E0:C_E0 + 1],
                                        ALU.mult, ALU.add))
            step(V.tensor_copy(EFF[:, 0:BANK], PS[:, 5, :]))
            step(V.tensor_copy(EFF[:, W_G:W_N], PS[:, 6, 0:2 * P]))
            split3(BROW[:, W_Z:W_N], PS[:, 6, 2 * P:3 * P], P, wk_bf, lambda ins: final(ins, norm_ready, 1))

            def normalise(t):
                dve.wait_ge(mm2_done, t * TG + TG)
                V.tensor_scalar(ve[0:96, :], PS[0:96, 4, :], EPS, None, ALU.add).then_inc(var_ready, 1)
                dve.wait_ge(std_ready, t + 2)
                r, w = rt[0:96, :], tmp[0:96, :]
                chain(t, V.reciprocal(r, sd[0:96, :]))
                chain(t, V.tensor_tensor(w, r, r, ALU.mult))
                chain(t, V.tensor_tensor(w, w, ve[0:96, :], ALU.mult))
                chain(t, V.tensor_scalar(w, w, -0.5, 1.5, ALU.mult, ALU.add))
                chain(t, V.tensor_tensor(r, r, w, ALU.mult))
                reached(dve, bc_done, t * TG)
                chain(t, V.tensor_copy(parts3[0:96, :], r))
                chain(t, V.tensor_tensor(r[32:64, :], r[32:64, :], parts3[32:64, :], ALU.subtract))
                chain(t, V.tensor_tensor(r[64:96, :], r[64:96, :], parts3[64:96, :], ALU.subtract))
                chain(t, V.tensor_copy(parts3[32:64, :], r[32:64, :]))
                chain(t, V.tensor_copy(parts3[64:96, :], r[64:96, :]))
                chain(t, V.tensor_tensor(r[64:96, :], r[64:96, :], parts3[64:96, :], ALU.subtract))
                V.tensor_copy(parts3[64:96, :], r[64:96, :]).then_inc(rb_ready, 1)
                for u in range(TG):
                    n = t * TG + u
                    dve.wait_ge(bc_done, n + 1)
                    tile = XT[:, ds(n * GR, GR), :].rearrange("p r n -> p (r n)")
                    V.tensor_tensor(tile, tile, PS[:, 5 + u % 2, :], ALU.mult).then_inc(zn_done, 1)

            CHAIN = 11
            made = [0]

            def chain(t, ins):
                made[0] += 1
                ins.then_inc(dve_chain, 1)
                dve.wait_ge(dve_chain, t * CHAIN + made[0])

            def normalise_round(t):
                made[0] = 0
                normalise(t)
                assert made[0] == CHAIN

            rounds(dve, normalise_round, NT, 1)

            for layer in range(2):
                base = NQ * NG * layer
                gate_sem = msk_done if layer == 0 else sig_done
                if layer == 1:
                    for s in range(2):
                        dve.wait_ge(xb_stored[s], 16 * (NB // 2))
                def chunk(q):
                    with dve.Fori(0, NG // 4) as g4:
                        for u in range(4):
                            n = q * NG + (g4 * 4 + u)
                            dve.wait_ge(gate_sem, n + 1 if layer == 0 else n + (base + 1))
                            v = PS[:, u, :].rearrange("p (r q k) -> p q k r", q=2, k=4 * CHUNK)
                            w = sig[:, u].rearrange("p (r q) k -> p q k r", q=2)
                            V.tensor_tensor(ab[:, :, :, ds(g4 * (4 * GR) + u * GR, GR)], v[:, :, 2 * CHUNK:4 * CHUNK, :],
                                            w, ALU.mult).then_inc(prod_done, 1)
                    for c in range(CHUNK):
                        s = (c // 2) % 2
                        dve.wait_ge(st_ready, q * CHUNK + (c + 1 + CH * layer))
                        if layer == 0:
                            reached(dve, acc_done, q * CHUNK + c)
                            V.tensor_tensor(S1[:, :], S1[:, :], st[:, s, :, c % 2], ALU.add).then_inc(s1_done, 1)
                            dve.wait_ge(sqp_ready, q * CHUNK + (c + 1))
                            dve.wait_ge(s1_done, q * CHUNK + (c + 1))
                            V.tensor_tensor(S2, S2, sqp, ALU.add).then_inc(acc_done, 1)
                        else:
                            V.bn_stats(REC[:, ds((q * CHUNK + c) * 6, 6)], st[:, s, :, c % 2]).then_inc(acc_done, 1)

                rounds(dve, chunk, NQ, 1 - layer)
                dve.wait_ge(acc_done, CH * (layer + 1))
                if layer == 0:
                    var, std, tmp_ = WK[:, 0:BANK], WK[:, BANK:2 * BANK], WK[:, 4 * BANK:5 * BANK]
                    for s in range(2):
                        dve.wait_ge(p_stored[s], 16 * (CH // 4))
                    step(V.tensor_scalar(S1[:, :], S1[:, :], 1.0 / CH, None, ALU.mult))
                    step(V.tensor_tensor(S1[:, :], S1[:, :], S1[:, :], ALU.mult))
                    step(V.scalar_tensor_tensor(var, S2, 1.0 / CH, S1[:, :], ALU.mult, ALU.subtract))
                    step(V.tensor_scalar(var, var, 0.0, None, ALU.max))
                    V.tensor_scalar(var, var, EPS, None, ALU.add).then_inc(var_ready, 1)
                    final(rsqrt(S1[:, :], var, std, NT + 2, tmp_), weights_ready, 1)
                else:
                    V.bn_aggr(T[:, 0:2], REC[:, :]).then_inc(small_in, 1)
                    answer()
                    step(V.tensor_scalar(col(2), PS[:, 7, 0:1], 1.0 / P, None, ALU.mult))
                    step(V.tensor_tensor(col(7), col(0), col(2), ALU.subtract))
                    V.scalar_tensor_tensor(col(3), col(7), col(7), col(1), ALU.mult, ALU.add).then_inc(small_in, 1)
                    answer()
                    V.tensor_scalar(col(4), PS[:, 7, 2:3], 1.0 / P, EPS, ALU.mult, ALU.add).then_inc(var_ready, 1)
                    step(rsqrt(col(6), col(4), col(5), NT + 5, col(7)))
                    step(V.tensor_tensor(col(6), col(6), VEC[:, V_AO:V_AO + 1], ALU.mult))
                    step(V.tensor_tensor(col(7), col(6), col(2), ALU.mult))
                    step(V.tensor_tensor(col(7), VEC[:, V_BO:V_BO + 1], col(7), ALU.subtract))
                    step(V.tensor_scalar(EFF[:, W_Z:W_N], RAW[:, W_Z:W_N], col(6), None, ALU.mult))
                    V.tensor_scalar(p_shift_all, ones, col(7), None, ALU.mult).then_inc(small_in, 1)
                    answer()
                    for s in range(2):
                        dve.wait_ge(p_stored[s], 16 * (CH // 4) * 2)
                    split3(BROW[:, W_Z:W_N], PS[:, 6, 0:P], P, wk_bf, lambda ins: final(ins, weights_ready, 2))

                base = NG * layer

                def finish_steps(g0, n_steps, lo):
                    for k in range(n_steps):
                        g = g0 + k
                        if lo[0] <= k < lo[1]:
                            s, u = (k // BG) % 2, k % BG
                            if u == 0:
                                dve.wait_ge(p_in[s], g0 * 4 + 64 * (1 + NB // 2 * layer))
                            reached(dve, tb_done, g + (base - 1))
                            for q in range(2):
                                src = ptb[:, s].rearrange("p (c q) (r e) -> p q c r e", q=2, e=2)
                                dst = pn[:, k % 2].rearrange("p r (q c e) -> p q c r e", q=2, e=2)
                                tile = src[:, q, :, u * GR:(u + 1) * GR, :]
                                if layer == 0:
                                    rs = rstd2[:, q, ds(g * GR, GR)].unsqueeze(1).unsqueeze(3)
                                    ins = V.tensor_tensor(dst[:, q], tile, rs.to_broadcast([P, CH // 2, GR, 2]),
                                                          ALU.mult)
                                else:
                                    ins = V.tensor_copy(dst[:, q], tile)
                            ins.then_inc(pn_done, 1)
                        if lo[2] <= k < lo[3]:
                            h = g - 2
                            dve.wait_ge(z_done, h + (1 + base))
                            dve.wait_ge(sg_done, h + (1 + base))
                            tile = sg[(k + 2) % 4]
                            V.tensor_tensor(tile, PS[:, 2 + k % 2, :], tile, ALU.mult).then_inc(y_done, 1)
                        if layer == 0 and lo[4] <= k < lo[5]:
                            h = g - 5
                            dve.wait_ge(x1t_ready, h + 1)
                            V.bn_stats(REC[:, ds(h * 6, 6)], XT[:, ds(h * GR, GR), :].rearrange("p r n -> p (r n)")
                                       ).then_inc(bn_done, 1)

                finish_steps(0, 16, (0, 16, 2, 16, 5, 16))
                with dve.Fori(1, NG // 16) as i:
                    finish_steps(i * 16, 16, (0, 16, 0, 16, 0, 16))
                finish_steps(NG, 5, (0, 0, 0, 2, 0, 5))

                if layer == 0:
                    dve.wait_ge(bn_done, 2 * NG)
                    dve.wait_ge(raw1_in, 16)
                    group_norm(NT + 3)
                    step(V.tensor_tensor(col(9), col(0), col(6), ALU.mult))
                    step(V.tensor_tensor(col(10), col(9), col(8), ALU.add))
                    step(V.tensor_tensor(col(11), col(6), col(6), ALU.mult))
                    V.tensor_tensor(col(11), col(11), col(1), ALU.mult).then_inc(small_in, 1)
                    answer()
                    step(V.tensor_scalar(col(9), PS[:, 7, 4:5], 1.0 / P, None, ALU.mult))
                    step(V.tensor_tensor(col(7), col(10), col(9), ALU.subtract))
                    V.scalar_tensor_tensor(col(12), col(7), col(7), col(11), ALU.mult, ALU.add).then_inc(small_in, 1)
                    answer()
                    V.tensor_scalar(col(16), PS[:, 7, 6:7], 1.0 / P, EPS, ALU.mult, ALU.add).then_inc(var_ready, 1)
                    step(rsqrt(col(13), col(16), col(17), NT + 4, col(7)))
                    step(V.tensor_tensor(col(13), col(13), VEC[:, V_AI:V_AI + 1], ALU.mult))
                    step(V.tensor_tensor(col(6), col(6), col(13), ALU.mult))
                    step(V.tensor_tensor(col(8), col(8), col(9), ALU.subtract))
                    step(V.scalar_tensor_tensor(col(8), col(8), col(13), VEC[:, V_BI:V_BI + 1], ALU.mult, ALU.add))
                    step(V.tensor_scalar(EFF[:, 0:W_Z], RAW[:, 0:W_Z], col(6), None, ALU.mult))
                    V.tensor_scalar(shift_all, ones, col(8), None, ALU.mult).then_inc(small_in, 1)
                    answer()
                    split3(BROW[:, 0:BANK], PS[:, 5, :], BANK, wk_bf)
                    split3(BROW[:, W_G:W_Z], PS[:, 6, 0:P], P, wk_bf, lambda ins: final(ins, norm_ready, 2))

    return nc


def shape_constants():
    k = np.arange(P)
    par, c = k // CH, k % CH
    same = (par[:, None] == par[None, :])
    eye = np.eye(P)
    consts = np.zeros((P, C_N))
    consts[:, C_ID:C_ID + P] = eye
    consts[:, C_GM:C_GM + P] = (c[:, None] // 2 == c[None, :] // 2) / 4
    consts[:, C_ONES:C_ONES + P] = 1
    consts[:, C_E0] = c == 0
    consts[:, C_NE0] = c != 0
    norm = np.zeros((P, L_N))
    norm[:, L_CM:L_CM + P] = eye - same / CH
    norm[:, L_DROP:L_DROP + P] = (eye - (same & (c[:, None] == 0))) * (c[None, :] != 0)
    for part in range(3):
        norm[k, L_SEL + 30 + 32 * part + par] = 1 / CH
    norm[k, L_ECOL + CH * par] = 1
    norm[0, L_BSEL] = 1
    norm[1, L_BSEL + CH] = 1
    spread = np.zeros((P, TG, P))
    for part in range(3):
        for u in range(TG):
            for q in range(2):
                spread[32 * part + 2 * u + q, u, (par == q) & (c != 0)] = 1
    spread[96, :, c == 0] = 1
    ones3 = np.zeros((P, P))
    ones3[[0, 32, 64]] = 1
    return consts, norm, spread.reshape(P, TG * P), ones3


def kernel(**inputs):
    import concourse.bacc as bacc
    from concourse.bass_utils import run_bass_kernel_spmd as run
    import ml_dtypes

    a = {k: np.asarray(v) for k, v in inputs.items()}

    def weights(gate_a, gate_b, lin_a, lin_b, gate_o, lin_o):
        four = np.stack([gate_a, gate_b, lin_a, lin_b], 1).reshape(CH, 4, NQ, CHUNK)
        four = four.transpose(0, 2, 1, 3).reshape(CH, NQ, CH)
        cols = np.concatenate([four, gate_o[:, None], lin_o[:, None]], 1)
        gap = np.zeros_like(cols)
        even = np.stack([cols, gap], 2).reshape(CH, W_N)
        odd = np.stack([gap, cols], 2).reshape(CH, W_N)
        return np.ascontiguousarray(np.concatenate([even, odd], 0))

    def biases(gate_a, gate_b, lin_a, lin_b, gate_o, lin_o):
        four = np.stack([gate_a, gate_b, lin_a, lin_b], 0).reshape(4, NQ, CHUNK)
        cols = np.concatenate([four.transpose(1, 0, 2).reshape(NQ, CH), gate_o[None], lin_o[None]], 0)
        gap = np.zeros_like(cols)
        return np.stack([np.stack([cols, gap], 1).reshape(W_N), np.stack([gap, cols], 1).reshape(W_N)], 0)

    L0, L1 = "L0_conv_", "L1_conv_"
    names0 = [L0 + n for n in ("w_ag", "w_bg", "w_ap", "w_bp", "w_g", "w_z")]
    names1 = [L1 + n for n in ("W_ga", "W_gb", "W_la", "W_lb", "W_go", "W_lo")]
    bias0 = [L0 + n for n in ("b_ag", "b_bg", "b_ap", "b_bp", "b_g", "b_z")]
    bias1 = [L1 + n for n in ("b_ga", "b_gb", "b_la", "b_lb", "b_go", "b_lo")]
    vecs = [np.concatenate([a[L0 + n]] * 2) for n in ("ln_in_w", "ln_in_b", "ln_out_w", "ln_out_b")]
    vecs += [np.repeat(a[L1 + n], P) for n in ("alpha_in", "beta_in", "alpha_o", "beta_o")]
    consts, norm, spread, ones3 = shape_constants()
    arrays = {
        "x": np.ascontiguousarray(a["x"]),
        "mask": np.ascontiguousarray(a[L0 + "mask"]),
        "w0": weights(*(a[n] for n in names0)),
        "w1": weights(*(a[n].T for n in names1)),
        "bias0": biases(*(a[n] for n in bias0)),
        "bias1": biases(*(a[n] for n in bias1)),
        "vecs": np.ascontiguousarray(np.stack(vecs, 1)),
        "consts": consts.astype(np.float32),
        "norm_consts": norm.astype(np.float32),
        "spread": spread.astype(ml_dtypes.bfloat16),
        "ones3": ones3.astype(ml_dtypes.bfloat16),
    }
    nc = bacc.Bacc("TRN2", target_bir_lowering=False, num_devices=1, dynamic_dma_scratch_size=64)
    args = [nc.dram_tensor(n, v.shape, mybir.dt.from_np(v.dtype), kind="ExternalInput").ap()
            for n, v in arrays.items()]
    out = nc.dram_tensor("out", (1, ROWS, COLS, CH), mybir.dt.float32, kind="ExternalOutput").ap()
    build(nc, *args, out)
    r = run(nc, [arrays], core_ids=[0])
    return r.results[0]["out"]
```

```python
import numpy as np
from contextlib import ExitStack

import concourse.bass as bass
from concourse import mybir

ROWS = 256
COLS = 256
CH = 64
P = 128
ROW = 2 * CH
GR = 4
NG = ROWS // GR
BANK = 512
CHUNK = 16
NQ = CH // CHUNK
LOAD_ROWS = 16
LOAD_SLOTS = 4
LG = LOAD_ROWS // GR
BR = 32
BG = BR // GR
NB = ROWS // BR
HR = 16
HG = HR // GR
HS = 4
AHEAD = 4
SPREAD_LAG = 5
TG = 16
NT = NG // TG
QW = 4 * 2 * CHUNK
W_G = NQ * QW
W_Z = W_G + ROW
W_N = W_Z + ROW
EPS = 1e-5
SEL = 32 * 2 + 2 + 2 * (TG - 1) + 30

C_ID, C_GM, C_ONES, C_E0, C_NE0, C_N = 0, 128, 256, 384, 385, 386
L_CM, L_DROP, L_SEL, L_ECOL, L_BSEL, L_N = 0, 128, 256, 384, 512, 640
V_LNW, V_LNB, V_OW, V_OB, V_AI, V_BI, V_AO, V_BO, V_N = range(9)


def build(nc, x, mask, w0, w1, bias0, bias1, vecs, consts, norm_consts, spread, ones3, out):
    f32 = mybir.dt.float32
    bf16 = mybir.dt.bfloat16
    ALU = mybir.AluOpType
    ACT = mybir.ActivationFunctionType
    ds = bass.ds

    x_tok = x[0].rearrange("r (p q) c -> p r (q c)", q=2)
    out_tok = out[0].rearrange("r (p q) c -> p r (q c)", q=2)
    p_dram = nc.dram_tensor("p_scratch", [P, CH // 2, 2 * ROWS * 2], f32, kind="Internal").ap()
    p_blocks = p_dram.rearrange("p c (q r e) -> p (c q) (r e)", q=2, e=2)
    x1_dram = nc.dram_tensor("x1_scratch", [P, ROWS, ROW], f32, kind="Internal").ap()

    ctx = ExitStack()
    with ctx:
        def sb(name, cols, dt=f32):
            return ctx.enter_context(nc.sbuf_tensor(name, [P, cols], dt))

        def sem(name):
            return ctx.enter_context(nc.semaphore(name))

        XT = ctx.enter_context(nc.sbuf_tensor("XT", [P, ROWS, P], f32))
        AB = sb("AB", 2 * 2 * CHUNK * ROWS)
        CF = sb("CF", C_N)
        RAW = sb("RAW", W_N)
        EFF = sb("EFF", W_N)
        BROW = sb("BROW", ROW, bf16)
        ONES3 = sb("ONES3", P, bf16)
        MS = sb("MS", 2 * BANK)
        S1 = sb("S1", BANK)
        WK = sb("WK", 7 * BANK)
        REC = sb("REC", 6 * NG)
        rows_tmp = sb("rows_tmp", 2 * ROWS // 4)
        VEC = sb("VEC", V_N)
        T = sb("T", 24)
        PS = ctx.enter_context(nc.psum_tensor("PS", [P, 8, BANK], f32))

        ident = CF[:, C_ID:C_ID + P]
        group_mean = CF[:, C_GM:C_GM + P]
        ones = CF[:, C_ONES:C_ONES + P]

        bias_all = RAW[:, 0:W_Z]
        shift_all = EFF[:, W_Z:W_N]

        xs = AB[:, 0:LOAD_SLOTS * LOAD_ROWS * ROW].rearrange("p (s r m) -> p s r m", s=LOAD_SLOTS, m=ROW)
        at = LOAD_SLOTS * LOAD_ROWS * ROW

        def part(n):
            nonlocal at
            at += n
            return AB[:, at - n:at]

        NCF = part(L_N)
        maskn = part(2 * COLS)
        brow0 = part(W_N)
        spread_sb = part(TG * P // 2).bitcast(bf16)
        sq = part(2 * BANK).rearrange("p (s n) -> p s n", s=2)
        ve, sd, rt, tmp = (part(BANK) for _ in range(4))
        parts3 = part(BANK // 2).bitcast(bf16)
        cs = part(P)
        wW = part(W_N)
        lnb_col = part(P)
        lnb_all = part(P)
        assert at <= 2 * 2 * CHUNK * ROWS
        ab = AB[:, :].rearrange("p (q k r) -> p q k r", q=2, r=ROWS)
        ptb = AB[:, 0:2 * CH * BR * 2].rearrange("p (s m n) -> p s m n", s=2, n=2 * BR)
        xb = AB[:, 2 * CH * BR * 2:4 * CH * BR * 2].rearrange("p (s r m) -> p s r m", s=HS, m=ROW)

        sig = WK[:, 0:4 * 256].rearrange("p (s t k) -> p s t k", s=4, k=2 * CHUNK)
        st = WK[:, 1024:1024 + 4 * BANK].rearrange("p (s n e) -> p s n e", s=2, e=2)
        sqp = WK[:, 6 * BANK:7 * BANK]
        biased = [WK[:, 0:BANK], WK[:, BANK:2 * BANK], WK[:, 6 * BANK:7 * BANK], S1[:, :]]
        pn = WK[:, 0:2 * BANK].rearrange("p (s r m) -> p s r m", s=2, m=ROW)
        pt = WK[:, 2 * BANK:4 * BANK].rearrange("p (s n) -> p s n", s=2)
        sg = [WK[:, 4 * BANK:5 * BANK], WK[:, 5 * BANK:6 * BANK], MS[:, 0:BANK], MS[:, BANK:2 * BANK]]
        maskT = MS[:, 0:BANK].rearrange("p (q r) -> p q r", q=2)
        S2 = MS[:, BANK:2 * BANK]
        brow1 = MS[:, 0:W_N]
        spare, spare_bf = WK[:, 0:P], WK[:, BANK:BANK + P // 2].bitcast(bf16)
        rstd2 = S1[:, :].rearrange("p (q r) -> p q r", q=2)

        ident_in = sem("ident_in")
        mask_in = sem("mask_in")
        consts_in = sem("consts_in")
        raw1_in = sem("raw1_in")
        brow1_in = sem("brow1_in")
        xs_in = [sem(f"xs_in{s}") for s in range(LOAD_SLOTS)]
        tr_done = sem("tr_done")
        xt_ready = sem("xt_ready")
        bn_done = sem("bn_done")
        mask_tr = sem("mask_tr")
        mask_ready = sem("mask_ready")
        dve_step = sem("dve_step")
        dve_chain = sem("dve_chain")
        s1_done = sem("s1_done")
        small_in = sem("small_in")
        small_out = sem("small_out")
        var_ready = sem("var_ready")
        std_ready = sem("std_ready")
        norm_ready = sem("norm_ready")
        folded = sem("folded")
        biases_ready = sem("biases_ready")
        weights_ready = sem("weights_ready")
        mm1_done = sem("mm1_done")
        zc_done = sem("zc_done")
        sq_ready = sem("sq_ready")
        mm2_done = sem("mm2_done")
        rb_zero = sem("rb_zero")
        rb_ready = sem("rb_ready")
        bc_done = sem("bc_done")
        zn_done = sem("zn_done")
        proj_done = [sem(f"proj_done{layer}") for layer in range(2)]
        sig_done = sem("sig_done")
        msk_done = sem("msk_done")
        bias_added = sem("bias_added")
        gate_bias_added = sem("gate_bias_added")
        prod_done = [sem(f"prod_done{layer}") for layer in range(2)]
        ein_done = sem("ein_done")
        st_ready = sem("st_ready")
        sqp_ready = sem("sqp_ready")
        acc_done = sem("acc_done")
        p_stored = [sem(f"p_stored{s}") for s in range(2)]
        p_in = [sem(f"p_in{s}") for s in range(2)]
        xb_in = [sem(f"xb_in{s}") for s in range(HS)]
        xb_stored = [sem(f"xb_stored{s}") for s in range(HS)]
        pn_done = sem("pn_done")
        tb_done = sem("tb_done")
        pt_ready = sem("pt_ready")
        g_done = sem("g_done")
        sg_done = sem("sg_done")
        z_done = sem("z_done")
        y_done = sem("y_done")
        xadd_done = sem("xadd_done")
        x1tr_done = sem("x1tr_done")
        x1t_ready = sem("x1t_ready")

        N_CONSTS = 6

        block = ctx.enter_context(nc.Block())

        def rounds(eng, body, n, peeled, last=None):
            for i in range(peeled):
                body(i)
            with eng.Fori(peeled, n if last is None else n - 1) as i:
                body(i)
            if last is not None:
                last(n - 1)

        def reached(eng, semaphore, value):
            if not isinstance(value, int) or value > 0:
                eng.wait_ge(semaphore, value)

        @block.sync
        def _(sp):
            def load_x(row, s):
                for h in range(2):
                    sp.dma_start(xs[:, s, h * LOAD_ROWS // 2:(h + 1) * LOAD_ROWS // 2, :],
                                 x_tok[:, ds(row + h * LOAD_ROWS // 2, LOAD_ROWS // 2), :]).then_inc(xs_in[s], 16)

            sp.dma_start(CF[:, :], consts).then_inc(ident_in, 16)
            load_x(0 * LOAD_ROWS, 0)
            load_x(1 * LOAD_ROWS, 1)
            sp.dma_start(maskn.rearrange("p (h c) -> p h c", h=2),
                         mask[0].rearrange("(h p) c -> p h c", h=2)).then_inc(mask_in, 16)
            load_x(2 * LOAD_ROWS, 2)
            load_x(3 * LOAD_ROWS, 3)
            with sp.Fori(1, ROWS // LOAD_ROWS // LOAD_SLOTS) as t4:
                for s in range(LOAD_SLOTS):
                    row = sp.snap(t4 * (LOAD_SLOTS * LOAD_ROWS) + s * LOAD_ROWS)
                    sp.wait_ge(tr_done, t4 * (LG * LOAD_SLOTS) + LG * (s + 1 - LOAD_SLOTS))
                    load_x(row, s)
            for dst, src in ((NCF, norm_consts), (VEC[:, :], vecs), (RAW[:, :], w0),
                             (brow0[0:2, :], bias0), (spread_sb, spread), (ONES3[:, :], ones3)):
                sp.dma_start(dst, src).then_inc(consts_in, 16)
            for layer in range(2):
                if layer == 0:
                    sp.wait_ge(small_out, 4)
                    sp.dma_start(RAW[:, :], w1).then_inc(raw1_in, 16)
                source, sink = (x_tok, x1_dram) if layer == 0 else (x1_dram, out_tok)

                def store_pair(q, pair):
                    at_pair = q * (CHUNK // 2) + pair
                    if not isinstance(q, int):
                        at_pair = sp.snap(at_pair)
                    sp.wait_ge(st_ready, q * CHUNK + (2 * pair + 2 + CH * layer))
                    sp.dma_start(p_dram[:, ds(at_pair, 1), :],
                                 st[:, pair % 2].rearrange("p n e -> p (n e)").unsqueeze(1)
                                 ).then_inc(p_stored[pair % 2], 16)

                def load_p(row, s, quarters):
                    for h in quarters:
                        sp.dma_start(ptb[:, s, h * CH // 4:(h + 1) * CH // 4, :],
                                     p_blocks[:, h * CH // 4:(h + 1) * CH // 4, ds(row * 2, 2 * BR)]
                                     ).then_inc(p_in[s], 16)

                def load_rows(row, s):
                    for h in range(2):
                        sp.dma_start(xb[:, s, h * HR // 2:(h + 1) * HR // 2, :],
                                     source[:, ds(row + h * HR // 2, HR // 2), :]).then_inc(xb_in[s], 16)

                def store_rows(row, s):
                    sp.dma_start(sink[:, ds(row, HR), :], xb[:, s]).then_inc(xb_stored[s], 16)

                with sp.Fori(0, NQ - 1) as q:
                    for pair in range(CHUNK // 2):
                        store_pair(q, pair)
                for pair in range(CHUNK // 2):
                    store_pair(NQ - 1, pair)
                    if pair == 1:
                        sp.wait_ge(ein_done, CH * layer + CH - CHUNK + 2 * pair + 2)
                        load_rows(0, 0)
                    if pair == 3:
                        sp.wait_ge(ein_done, CH * layer + CH - CHUNK + 2 * pair + 2)
                        for s in range(2):
                            sp.wait_ge(p_stored[s], 16 * (CH // 4 * layer + (CH - CHUNK) // 4))
                    if 3 <= pair < 6:
                        load_p(0, 0, (pair - 3,))
                for s in range(2):
                    sp.wait_ge(p_stored[s], 16 * (CH // 4) * (layer + 1))
                load_p(0, 0, (3,))
                load_rows(HR, 1)
                load_p(BR, 1, range(4))
                load_rows(2 * HR, 2)
                load_rows(3 * HR, 3)

                def block(b2, s, more):
                    for h in range(2):
                        slot = 2 * s + h
                        if isinstance(b2, int):
                            row = b2 * (2 * BR) + s * BR + h * HR
                            row_in, p_row = row + HS * HR, row + 2 * BR
                            groups = (row + HR) // GR + NG * layer
                            stores = 16 * (b2 + 1 + NB // 2 * layer)
                        else:
                            row = sp.snap(b2 * (2 * BR) + (s * BR + h * HR))
                            row_in = sp.snap(b2 * (2 * BR) + (s * BR + h * HR + HS * HR))
                            p_row = sp.snap(b2 * (2 * BR) + (s * BR + 2 * BR))
                            groups = sp.snap(b2 * (2 * BG) + ((s * BR + h * HR + HR) // GR + NG * layer))
                            tiles = sp.snap(b2 * (2 * BG) + ((s + 1) * BG + NG * layer))
                            stores = sp.snap(b2 * 16 + 16 * (1 + NB // 2 * layer))
                        sp.wait_ge(xadd_done, groups)
                        store_rows(row, slot)
                        if more:
                            if h == 0:
                                sp.wait_ge(tb_done, tiles)
                                load_p(p_row, s, range(4))
                            sp.wait_ge(xb_stored[slot], stores)
                            if layer == 0:
                                sp.wait_ge(x1tr_done, groups)
                            load_rows(row_in, slot)

                with sp.Fori(0, NB // 2 - 1) as b2:
                    for s in range(2):
                        block(b2, s, True)
                for s in range(2):
                    block(NB // 2 - 1, s, False)
                if layer == 0:
                    sp.wait_ge(xadd_done, NG)
                    sp.dma_start(brow1[0:2, :], bias1).then_inc(brow1_in, 16)
                for s in range(HS):
                    sp.wait_ge(xb_stored[s], 16 * (NB // 2) * (layer + 1))

        @block.tensor
        def _(pe):
            def mm(dst, lhsT, rhs, start=True, stop=True):
                return nc.tensor.matmul(dst, lhsT, rhs, start=start, stop=stop)

            pe.wait_ge(ident_in, 16)

            def transpose_loads(t4):
                for s in range(LOAD_SLOTS):
                    for u in range(LG):
                        g = s * LG + u
                        if u == 0:
                            pe.wait_ge(xs_in[s], t4 * 32 + 32)
                        reached(pe, xt_ready, t4 * (LG * LOAD_SLOTS) + (g - 3))
                        for r in range(GR):
                            last = nc.tensor.transpose(PS[:, g % 4, r * P:(r + 1) * P], xs[:, s, u * GR + r, :], ident)
                        last.then_inc(tr_done, 1)

            transpose_loads(0)
            pe.wait_ge(mask_in, 16)
            for q in range(2):
                for h in range(2):
                    src = maskn.rearrange("p (h c q) -> p h q c", h=2, q=2)[:, h, q]
                    last = nc.tensor.transpose(PS[:, 7, (2 * q + h) * P:(2 * q + h + 1) * P], src, ident)
            last.then_inc(mask_tr, 1)
            with pe.Fori(1, ROWS // LOAD_ROWS // LOAD_SLOTS) as t4:
                transpose_loads(t4)

            smalls = [0]

            def small(pairs):
                smalls[0] += 1
                pe.wait_ge(small_in, smalls[0])
                for args in pairs:
                    last = mm(*args)
                last.then_inc(small_out, 1)

            pe.wait_ge(mask_ready, 1)
            small([(PS[:, 7, 0:1], group_mean, T[:, 0:1])])
            small([(PS[:, 7, 2:3], group_mean, T[:, 3:4])])
            pe.wait_ge(consts_in, 16 * N_CONSTS)
            cm, drop = NCF[:, L_CM:L_CM + P], NCF[:, L_DROP:L_DROP + P]
            bsel = NCF[0:2, L_BSEL:L_BSEL + P]
            small([(PS[:, 7, 4:5], cm, T[:, 8:9])])

            def fold_weights():
                small([(PS[:, 5, :], drop, wW[:, 0:BANK], True, False),
                       (PS[:, 5, :], lnb_col, RAW[:, 0:BANK], False, False),
                       (PS[:, 5, :], bsel, brow0[0:2, 0:BANK], False, True),
                       (PS[:, 6, 0:P], drop, wW[:, W_G:W_Z], True, False),
                       (PS[:, 6, 0:P], lnb_col, RAW[:, W_G:W_Z], False, False),
                       (PS[:, 6, 0:P], bsel, brow0[0:2, W_G:W_Z], False, True),
                       (PS[:, 6, P:2 * P], cm, wW[:, W_Z:W_N]),
                       (PS[:, 6, 2 * P:3 * P], lnb_all, RAW[:, W_Z:W_N], True, False),
                       (PS[:, 6, 2 * P:3 * P], ones[0:2, :], brow0[0:2, W_Z:W_N], False, True)])

            def spread_rstd(t, u):
                if u == 0:
                    pe.wait_ge(rb_ready, t + 1)
                reached(pe, zn_done, t * TG + max(u - 1, 0))
                mm(PS[:, 5 + u % 2, :], spread_sb[:, u * P:(u + 1) * P], parts3).then_inc(bc_done, 1)

            def round_(t):
                spread = 0
                for u in range(TG + 1):
                    if u < TG:
                        reached(pe, sq_ready, t * TG + (u - 3))
                        mm(PS[:, u % 4, :], cs, XT[:, ds(t * (TG * GR) + u * GR, GR), :].rearrange("p r n -> p (r n)")
                           ).then_inc(mm1_done, 1)
                    if u >= 1:
                        v = u - 1
                        pe.wait_ge(sq_ready, t * TG + (v + 1))
                        if v == 0:
                            reached(pe, var_ready, t + 1)
                        s0 = L_SEL + 30 - 2 * v
                        mm(PS[0:96, 4, :], NCF[:, s0:s0 + 96], sq[:, v % 2], v == 0, v == TG - 1).then_inc(mm2_done, 1)
                    if isinstance(t, int) and t == 0:
                        if u == SPREAD_LAG:
                            fold_weights()
                    elif SPREAD_LAG <= u < TG:
                        for _ in range(1 if (u - SPREAD_LAG) % 2 or u == TG - 1 else 2):
                            spread_rstd(t - 1, spread)
                            spread += 1
                assert spread in (0, TG)

            rounds(pe, round_, NT, 2)
            for layer in range(2):
                free = sqp_ready if layer == 0 else st_ready

                def project(q, g):
                    bank = PS[:, g % 4, :]
                    n = q * NG + (g - 3)
                    if layer == 0:
                        reached(pe, prod_done[0], n)
                    else:
                        reached(pe, bias_added, n)
                    for r in range(GR):
                        last = mm(bank[:, r * QW:(r + 1) * QW], XT[:, g * GR + r, :], EFF[:, ds(q * QW, QW)])
                    last.then_inc(proj_done[layer], 1)

                def chunk(q):
                    for g in range(AHEAD, NG):
                        project(q, g)
                    for g in range(AHEAD):
                        project(q + 1, g)
                    pe.wait_ge(prod_done[layer], q * NG + NG)
                    for c in range(CHUNK):
                        reached(pe, free, q * CHUNK + (max(c - 3, 0) + CH * layer))
                        for jq in range(2):
                            for kq in range(2):
                                last = mm(PS[:, 4 + c % 4, jq * ROWS:(jq + 1) * ROWS],
                                          ab[:, kq, 2 * c + 1, jq::2], ab[:, kq, 2 * c, :], kq == 0, kq == 1)
                        last.then_inc(ein_done, 1)

                pe.wait_ge(folded, layer + 1)
                for g in range(AHEAD):
                    project(0, g)
                if layer == 0:
                    for u in range(TG):
                        spread_rstd(NT - 1, u)
                    pe.wait_ge(zn_done, NG)
                else:
                    pe.wait_ge(brow1_in, 16)
                    small([(PS[:, 5, :], shift_all, RAW[:, 0:BANK], True, False),
                           (PS[:, 5, :], ones[0:2, :], brow1[0:2, 0:BANK], False, True),
                           (PS[:, 6, 0:P], shift_all, RAW[:, W_G:W_Z], True, False),
                           (PS[:, 6, 0:P], ones[0:2, :], brow1[0:2, W_G:W_Z], False, True),
                           (PS[:, 6, P:2 * P], ones[0:2, :], brow1[0:2, W_Z:W_N])])
                    pe.wait_ge(biases_ready, 1)
                rounds(pe, chunk, NQ, 1 - layer)

                if layer == 1:
                    small([(PS[:, 7, 0:1], ones, T[:, 0:1])])
                    small([(PS[:, 7, 2:3], ones, T[:, 3:4])])
                w_out = (EFF if layer == 0 else RAW)[:, W_Z:W_N]
                base = NG * layer
                pe.wait_ge(free, CH * (layer + 1) if layer == 1 else CH)
                for step in range(NG + 3):
                    g = step
                    if g < NG:
                        pe.wait_ge(pn_done, base + g + 1)
                        reached(pe, pt_ready, base + g - 1)
                        for r in range(GR):
                            last = nc.tensor.transpose(PS[:, 4 + g % 2, r * P:(r + 1) * P], pn[:, g % 2, r, :], ident)
                        last.then_inc(tb_done, 1)
                    if AHEAD <= g < NG:
                        pe.wait_ge(sg_done if layer == 0 else gate_bias_added, g - 1)
                        for r in range(GR):
                            last = mm(PS[:, g % 2, r * P:(r + 1) * P], XT[:, g * GR + r, :], EFF[:, W_G:W_Z])
                        last.then_inc(g_done, 1)
                    g = step - 1
                    if 0 <= g < NG:
                        pe.wait_ge(pt_ready, base + g + 1)
                        reached(pe, y_done, base + g - 1)
                        bank = PS[:, 6 + g % 2, :]
                        mm(bank, ONES3[:, :], BROW[:, :].unsqueeze(1).to_broadcast([P, GR, ROW]), True, False)
                        for r in range(GR):
                            last = mm(bank[:, r * P:(r + 1) * P], pt[:, g % 2, r * P:(r + 1) * P], w_out,
                                      False, r == GR - 1)
                        last.then_inc(z_done, 1)
                    g = step - 3
                    if layer == 0 and 0 <= g < NG:
                        pe.wait_ge(xadd_done, g + 1)
                        if g < 2:
                            pe.wait_ge(sg_done, g + 3)
                        reached(pe, x1t_ready, g - 1)
                        for r in range(GR):
                            row = g * GR + r
                            last = nc.tensor.transpose(PS[:, 2 + g % 2, r * P:(r + 1) * P],
                                                       xb[:, row // HR % HS, row % HR, :], ident)
                        last.then_inc(x1tr_done, 1)

                if layer == 0:
                    pe.wait_ge(x1t_ready, NG)
                    small([(PS[:, 7, 0:1], group_mean, T[:, 0:1])])
                    small([(PS[:, 7, 2:3], group_mean, T[:, 3:4])])
                    small([(PS[:, 7, 4:6], ones, T[:, 10:12])])

        @block.scalar
        def _(act):
            def transposed(t4):
                for g in range(LG * LOAD_SLOTS):
                    n = t4 * (LG * LOAD_SLOTS) + g
                    act.wait_ge(tr_done, n + 1)
                    nc.scalar.activation(XT[:, ds(n * GR, GR), :].rearrange("p r n -> p (r n)"), PS[:, g % 4, :],
                                         ACT.Copy).then_inc(xt_ready, 1)

            transposed(0)
            act.wait_ge(mask_tr, 1)
            nc.scalar.activation(maskT.rearrange("p q r -> p (q r)"), PS[:, 7, :], ACT.Copy).then_inc(mask_ready, 1)
            with act.Fori(1, ROWS // LOAD_ROWS // LOAD_SLOTS) as t4:
                transposed(t4)

            def root(n, dst, src):
                act.wait_ge(var_ready, n)
                nc.scalar.activation(dst, src, ACT.Sqrt).then_inc(std_ready, 1)

            root(1, T[:, 5:6], T[:, 4:5])
            act.wait_ge(norm_ready, 1)

            def centred(t):
                for u in range(TG):
                    n = t * TG + u
                    act.wait_ge(mm1_done, n + 1)
                    nc.scalar.activation(XT[:, ds(n * GR, GR), :].rearrange("p r n -> p (r n)"), PS[:, u % 4, :],
                                         ACT.Identity, bias=T[:, 15:16], scale=CF[:, C_NE0:C_NE0 + 1]
                                         ).then_inc(zc_done, 1)
                    reached(act, mm2_done, n - 1)
                    nc.scalar.activation(sq[:, u % 2], PS[:, u % 4, :], ACT.Square, bias=T[:, 14:15]
                                         ).then_inc(sq_ready, 1)
                root(t + 2, sd[0:96, :], ve[0:96, :])

            centred(0)
            with act.Fori(1, NT) as t:
                centred(t)

            for layer in range(2):
                base = NQ * NG * layer

                def gates(q, g4):
                    for u in range(4):
                        n = q * NG + (g4 * 4 + u)
                        if layer == 0:
                            act.wait_ge(proj_done[0], n + 1)
                            reached(act, prod_done[0], n - 3)
                            nc.scalar.activation(
                                sig[:, u], PS[:, u, :].rearrange("p (t k) -> p t k", k=4 * CHUNK)[:, :, 0:2 * CHUNK],
                                ACT.Sigmoid).then_inc(sig_done, 1)
                        else:
                            act.wait_ge(bias_added, n + 1)
                            tile = biased[u].rearrange("p (t k) -> p t k", k=4 * CHUNK)[:, :, 0:2 * CHUNK]
                            nc.scalar.activation(tile, tile, ACT.Sigmoid).then_inc(sig_done, 1)

                def chunk(q, last=False):
                    with act.Fori(1, NG // 4) as g4:
                        gates(q, g4)
                    if not last:
                        gates(q + 1, 0)
                    for c in range(CHUNK):
                        s = (c // 2) % 2
                        act.wait_ge(ein_done, q * CHUNK + (c + 1 + CH * layer))
                        if c % 2 == 0:
                            reached(act, p_stored[s], q * (16 * CHUNK // 4) + 16 * (c // 4 + CH // 4 * layer))
                            reached(act, acc_done, q * CHUNK + (max(c - 2, 0) + CH * layer))
                        nc.scalar.activation(st[:, s, :, c % 2], PS[:, 4 + c % 4, :], ACT.Copy).then_inc(st_ready, 1)
                        if layer == 0:
                            reached(act, acc_done, q * CHUNK + c)
                            nc.scalar.activation(sqp, PS[:, 4 + c % 4, :], ACT.Square).then_inc(sqp_ready, 1)

                gates(0, 0)
                rounds(act, chunk, NQ, 1 - layer, lambda q: chunk(q, last=True))

                base = NG * layer
                if layer == 0:
                    root(NT + 2, S1[:, :], sqp)
                else:
                    root(NT + 5, T[:, 5:6], T[:, 4:5])
                act.wait_ge(weights_ready, layer + 1)
                for s in range(2):
                    act.wait_ge(p_stored[s], 16 * (CH // 4) * (layer + 1))

                def finish_steps(g0, n_steps, lo):
                    for k in range(n_steps):
                        g = g0 + k
                        if lo[0] <= k < lo[1]:
                            act.wait_ge(tb_done, g + (1 + base))
                            reached(act, z_done, g + (base - 1))
                            if layer == 1:
                                nc.scalar.activation(pt[:, k % 2], PS[:, 4 + k % 2, :], ACT.Identity,
                                                     bias=T[:, 8:9], scale=T[:, 6:7]).then_inc(pt_ready, 1)
                            else:
                                nc.scalar.activation(pt[:, k % 2], PS[:, 4 + k % 2, :], ACT.Copy
                                                     ).then_inc(pt_ready, 1)
                                ahead = isinstance(g, int) and g < AHEAD
                                if ahead:
                                    act.wait_ge(proj_done[0], NQ * NG + g + 1)
                                else:
                                    act.wait_ge(g_done, g - (AHEAD - 1))
                                reached(act, xadd_done, g - 3)
                                nc.scalar.activation(sg[k % 4], PS[:, k if ahead else k % 2, :], ACT.Sigmoid
                                                     ).then_inc(sg_done, 1)
                        if layer == 1 and lo[2] <= k < lo[3]:
                            act.wait_ge(gate_bias_added, g)
                            tile = sg[(k - 1) % 4]
                            nc.scalar.activation(tile, tile, ACT.Sigmoid).then_inc(sg_done, 1)
                        if layer == 0 and lo[2] <= k < lo[3]:
                            h = g - 4
                            act.wait_ge(x1tr_done, h + 1)
                            nc.scalar.activation(XT[:, ds(h * GR, GR), :].rearrange("p r n -> p (r n)"),
                                                 PS[:, 2 + k % 2, :], ACT.Copy).then_inc(x1t_ready, 1)

                first = 4 if layer == 0 else 1
                finish_steps(0, 16, (0, 16, first, 16))
                with act.Fori(1, NG // 16) as i:
                    finish_steps(i * 16, 16, (0, 16, 0, 16))
                finish_steps(NG, first, (0, 0, 0, first))
                if layer == 0:
                    root(NT + 3, T[:, 5:6], T[:, 4:5])
                    root(NT + 4, T[:, 17:18], T[:, 16:17])

        @block.gpsimd
        def _(pool):
            pool.wait_ge(mask_ready, 1)

            with pool.Fori(0, NQ) as q:
                with pool.Fori(0, NG // 4) as g4:
                    for u in range(4):
                        pool.wait_ge(sig_done, q * NG + (g4 * 4 + (u + 1)))
                        rows = maskT[:, :, ds(g4 * (4 * GR) + u * GR, GR)].rearrange("p q r -> p r q")
                        tile = sig[:, u].rearrange("p (r q) k -> p r q k", q=2)
                        nc.gpsimd.tensor_tensor(tile, tile, rows.unsqueeze(3).to_broadcast([P, GR, 2, 2 * CHUNK]),
                                                ALU.mult).then_inc(msk_done, 1)
            for layer in range(2):
                if layer == 1:
                    def products(q, g4):
                        for u in range(4):
                            n = q * NG + (g4 * 4 + u)
                            pool.wait_ge(sig_done, n + (1 + NQ * NG))
                            v = biased[u].rearrange("p (r q k) -> p q k r", q=2, k=4 * CHUNK)
                            nc.gpsimd.tensor_tensor(ab[:, :, :, ds(g4 * (4 * GR) + u * GR, GR)], v[:, :, 2 * CHUNK:4 * CHUNK, :],
                                                    v[:, :, 0:2 * CHUNK, :], ALU.mult).then_inc(prod_done[1], 1)

                    for s in range(HS):
                        pool.wait_ge(xb_stored[s], 16 * (NB // 2))
                    with pool.Fori(0, NQ) as q:
                        pool.wait_ge(ein_done, q * CHUNK + CH)
                        products(q, 0)
                        with pool.Fori(1, NG // 4) as g4:
                            products(q, g4)
                base = NG * layer
                with pool.Fori(0, NB // 2) as b2:
                    for s in range(HS):
                        pool.wait_ge(xb_in[s], b2 * 32 + 32 * (1 + NB // 2 * layer))
                        for u in range(HG):
                            g = s * HG + u
                            pool.wait_ge(y_done, b2 * (2 * BG) + (g + 1 + base))
                            rows = xb[:, s, u * GR:(u + 1) * GR, :].rearrange("p r m -> p (r m)")
                            nc.gpsimd.tensor_tensor(rows, rows, sg[g % 4], ALU.add).then_inc(xadd_done, 1)

        @block.vector
        def _(dve):
            steps = [0]
            counts = {"small": 0}

            def step(ins):
                steps[0] += 1
                ins.then_inc(dve_step, 1)
                dve.wait_ge(dve_step, steps[0])

            def answer():
                counts["small"] += 1
                dve.wait_ge(small_out, counts["small"])

            def col(i):
                return T[:, i:i + 1]

            V = nc.vector

            def final(ins, semaphore, value):
                ins.then_inc(semaphore, 1)
                dve.wait_ge(semaphore, value)

            def rsqrt(dst, var, std, n, tmp_):
                dve.wait_ge(std_ready, n)
                step(V.reciprocal(dst, std))
                step(V.scalar_tensor_tensor(tmp_, dst, -0.5, dst, ALU.mult, ALU.mult))
                step(V.tensor_tensor(tmp_, tmp_, var, ALU.mult))
                return V.scalar_tensor_tensor(dst, tmp_, 1.5, dst, ALU.add, ALU.mult)

            def group_norm(n):
                V.bn_aggr(T[:, 0:2], REC[:, :]).then_inc(small_in, 1)
                answer()
                step(V.tensor_copy(col(2), PS[:, 7, 0:1]))
                step(V.tensor_tensor(col(7), col(0), col(2), ALU.subtract))
                V.scalar_tensor_tensor(col(3), col(7), col(7), col(1), ALU.mult, ALU.add).then_inc(small_in, 1)
                answer()
                V.tensor_scalar(col(4), PS[:, 7, 2:3], EPS, None, ALU.add).then_inc(var_ready, 1)
                step(rsqrt(col(6), col(4), col(5), n, col(7)))
                step(V.scalar_tensor_tensor(col(8), col(2), -1.0, col(6), ALU.mult, ALU.mult))

            def split3(dst, src, done):
                step(V.tensor_copy(dst[0:1, :], src[0:1, :]))
                step(V.tensor_copy(spare_bf, src))
                step(V.tensor_tensor(spare, src, spare_bf, ALU.subtract))
                step(V.tensor_copy(dst[32:33, :], spare[32:33, :]))
                step(V.tensor_copy(spare_bf, spare))
                step(V.tensor_tensor(spare, spare, spare_bf, ALU.subtract))
                done(V.tensor_copy(dst[64:65, :], spare[64:65, :]))

            step(V.memset(BROW[:, :], 0.0))
            step(V.memset(S1[:, :], 0.0))
            step(V.memset(S2, 0.0))
            step(V.memset(parts3[96:P, :], 1.0))

            def record(t4):
                for g in range(LG * LOAD_SLOTS):
                    n = t4 * (LG * LOAD_SLOTS) + g
                    dve.wait_ge(xt_ready, n + 1)
                    V.bn_stats(REC[:, ds(n * 6, 6)], XT[:, ds(n * GR, GR), :].rearrange("p r n -> p (r n)")
                               ).then_inc(bn_done, 1)

            with dve.Fori(0, ROWS // LOAD_ROWS // LOAD_SLOTS) as t4:
                record(t4)
            dve.wait_ge(bn_done, NG)
            group_norm(1)
            dve.wait_ge(consts_in, 16 * N_CONSTS)
            V.tensor_scalar(cs, NCF[:, L_CM:L_CM + P], col(6), None, ALU.mult).then_inc(small_in, 1)
            answer()
            step(V.tensor_copy(col(14), PS[:, 7, 4:5]))
            final(V.scalar_tensor_tensor(col(15), col(14), CF[:, C_NE0:C_NE0 + 1], CF[:, C_E0:C_E0 + 1],
                                         ALU.mult, ALU.add), norm_ready, 1)
            step(V.tensor_scalar(wW[:, 0:W_Z], RAW[:, 0:W_Z], VEC[:, V_LNW:V_LNW + 1], None, ALU.mult))
            step(V.tensor_scalar(wW[:, W_Z:W_N], RAW[:, W_Z:W_N], VEC[:, V_OW:V_OW + 1], None, ALU.mult))
            step(V.tensor_scalar(lnb_col, NCF[:, L_ECOL:L_ECOL + P], VEC[:, V_LNB:V_LNB + 1], None, ALU.mult))
            V.tensor_scalar(lnb_all, ones, VEC[:, V_OB:V_OB + 1], None, ALU.mult).then_inc(small_in, 1)
            answer()
            step(V.tensor_copy(EFF[:, 0:BANK], PS[:, 5, :]))
            step(V.tensor_copy(EFF[:, W_G:W_N], PS[:, 6, 0:2 * P]))
            split3(BROW[:, :], PS[:, 6, 2 * P:3 * P], lambda ins: final(ins, folded, 1))

            def normalise(t):
                dve.wait_ge(mm2_done, t * TG + TG)
                V.tensor_scalar(ve[0:96, :], PS[0:96, 4, :], EPS, None, ALU.add).then_inc(var_ready, 1)
                dve.wait_ge(std_ready, t + 2)
                r, w = rt[0:96, :], tmp[0:96, :]
                chain(t, V.reciprocal(r, sd[0:96, :]))
                chain(t, V.scalar_tensor_tensor(w, r, -0.5, r, ALU.mult, ALU.mult))
                chain(t, V.tensor_tensor(w, w, ve[0:96, :], ALU.mult))
                chain(t, V.scalar_tensor_tensor(r, w, 1.5, r, ALU.add, ALU.mult))
                reached(dve, bc_done, t * TG)
                chain(t, V.tensor_copy(parts3[0:96, :], r))
                chain(t, V.tensor_tensor(r[32:64, :], r[32:64, :], parts3[32:64, :], ALU.subtract))
                chain(t, V.tensor_tensor(r[64:96, :], r[64:96, :], parts3[64:96, :], ALU.subtract))
                chain(t, V.tensor_copy(parts3[32:64, :], r[32:64, :]))
                chain(t, V.tensor_copy(parts3[64:96, :], r[64:96, :]))
                chain(t, V.tensor_tensor(r[64:96, :], r[64:96, :], parts3[64:96, :], ALU.subtract))
                V.tensor_copy(parts3[64:96, :], r[64:96, :]).then_inc(rb_ready, 1)
                for u in range(TG):
                    n = t * TG + u
                    dve.wait_ge(bc_done, n + 1)
                    tile = XT[:, ds(n * GR, GR), :].rearrange("p r n -> p (r n)")
                    V.tensor_tensor(tile, tile, PS[:, 5 + u % 2, :], ALU.mult).then_inc(zn_done, 1)

            CHAIN = 10
            made = [0]

            def chain(t, ins):
                made[0] += 1
                ins.then_inc(dve_chain, 1)
                dve.wait_ge(dve_chain, t * CHAIN + made[0])

            def normalise_round(t):
                made[0] = 0
                normalise(t)
                assert made[0] == CHAIN

            rounds(dve, normalise_round, NT, 1)

            for layer in range(2):
                def products(q, g4):
                    for u in range(4):
                        n = q * NG + (g4 * 4 + u)
                        dve.wait_ge(msk_done, n + 1)
                        v = PS[:, u, :].rearrange("p (r q k) -> p q k r", q=2, k=4 * CHUNK)
                        w = sig[:, u].rearrange("p (r q) k -> p q k r", q=2)
                        V.tensor_tensor(ab[:, :, :, ds(g4 * (4 * GR) + u * GR, GR)], v[:, :, 2 * CHUNK:4 * CHUNK, :],
                                        w, ALU.mult).then_inc(prod_done[0], 1)

                def add_biases(q, g4):
                    for u in range(4):
                        n = q * NG + (g4 * 4 + u)
                        dve.wait_ge(proj_done[1], n + 1)
                        reached(dve, prod_done[1], n - 3)
                        bias = bias_all[:, ds(q * QW, QW)].unsqueeze(1).to_broadcast([P, GR, QW])
                        V.tensor_tensor(biased[u].rearrange("p (r m) -> p r m", m=QW),
                                        PS[:, u, :].rearrange("p (r m) -> p r m", m=QW), bias, ALU.add
                                        ).then_inc(bias_added, 1)

                def chunk(q, last=False):
                    if layer == 0:
                        with dve.Fori(0, NG // 4) as g4:
                            products(q, g4)
                    else:
                        with dve.Fori(1, NG // 4) as g4:
                            add_biases(q, g4)
                        if not last:
                            add_biases(q + 1, 0)
                    for c in range(CHUNK):
                        s = (c // 2) % 2
                        dve.wait_ge(st_ready, q * CHUNK + (c + 1 + CH * layer))
                        if layer == 0:
                            reached(dve, acc_done, q * CHUNK + c)
                            V.tensor_tensor(S1[:, :], S1[:, :], st[:, s, :, c % 2], ALU.add).then_inc(s1_done, 1)
                            dve.wait_ge(sqp_ready, q * CHUNK + (c + 1))
                            dve.wait_ge(s1_done, q * CHUNK + (c + 1))
                            V.tensor_tensor(S2, S2, sqp, ALU.add).then_inc(acc_done, 1)
                        else:
                            V.bn_stats(REC[:, ds((q * CHUNK + c) * 6, 6)], st[:, s, :, c % 2]).then_inc(acc_done, 1)

                if layer == 0:
                    rounds(dve, chunk, NQ, 1)
                else:
                    add_biases(0, 0)
                    rounds(dve, chunk, NQ, 0, lambda q: chunk(q, last=True))
                dve.wait_ge(acc_done, CH * (layer + 1))
                if layer == 0:
                    var = sqp
                    step(V.scalar_tensor_tensor(S1[:, :], S1[:, :], 1.0 / CH ** 2, S1[:, :], ALU.mult, ALU.mult))
                    step(V.scalar_tensor_tensor(var, S2, 1.0 / CH, S1[:, :], ALU.mult, ALU.subtract))
                    V.tensor_scalar(var, var, 0.0, EPS, ALU.max, ALU.add).then_inc(var_ready, 1)
                    dve.wait_ge(std_ready, NT + 2)

                    def rstd_rows(i):
                        def rows(tile):
                            return tile.rearrange("p (q r) -> p q r", q=2)[:, :, i * ROWS // 4:(i + 1) * ROWS // 4]

                        r, w = rows(S1[:, :]), rows_tmp[:, :].rearrange("p (q r) -> p q r", q=2)
                        step(V.reciprocal(r, r))
                        step(V.scalar_tensor_tensor(w, r, -0.5, r, ALU.mult, ALU.mult))
                        step(V.tensor_tensor(w, w, rows(var), ALU.mult))
                        return V.scalar_tensor_tensor(r, w, 1.5, r, ALU.add, ALU.mult)

                    final(rstd_rows(0), weights_ready, 1)
                else:
                    V.bn_aggr(T[:, 0:2], REC[:, :]).then_inc(small_in, 1)
                    answer()
                    step(V.tensor_scalar(col(2), PS[:, 7, 0:1], 1.0 / P, None, ALU.mult))
                    step(V.tensor_tensor(col(7), col(0), col(2), ALU.subtract))
                    V.scalar_tensor_tensor(col(3), col(7), col(7), col(1), ALU.mult, ALU.add).then_inc(small_in, 1)
                    answer()
                    V.tensor_scalar(col(4), PS[:, 7, 2:3], 1.0 / P, EPS, ALU.mult, ALU.add).then_inc(var_ready, 1)
                    step(rsqrt(col(6), col(4), col(5), NT + 5, col(7)))
                    step(V.tensor_tensor(col(6), col(6), VEC[:, V_AO:V_AO + 1], ALU.mult))
                    step(V.tensor_tensor(col(7), col(6), col(2), ALU.mult))
                    final(V.tensor_tensor(col(8), VEC[:, V_BO:V_BO + 1], col(7), ALU.subtract), weights_ready, 2)
                    for s in range(2):
                        dve.wait_ge(p_stored[s], 16 * (CH // 4) * 2)

                base = NG * layer

                def finish_steps(g0, n_steps, lo):
                    for k in range(n_steps):
                        g = g0 + k
                        if lo[0] <= k < lo[1]:
                            s, u = (k // BG) % 2, k % BG
                            if u == 0:
                                dve.wait_ge(p_in[s], g0 * 4 + 64 * (1 + NB // 2 * layer))
                            reached(dve, tb_done, g + (base - 1))
                            for q in range(2):
                                src = ptb[:, s].rearrange("p (c q) (r e) -> p q c r e", q=2, e=2)
                                dst = pn[:, k % 2].rearrange("p r (q c e) -> p q c r e", q=2, e=2)
                                tile = src[:, q, :, u * GR:(u + 1) * GR, :]
                                if layer == 0:
                                    rs = rstd2[:, q, ds(g * GR, GR)].unsqueeze(1).unsqueeze(3)
                                    ins = V.tensor_tensor(dst[:, q], tile, rs.to_broadcast([P, CH // 2, GR, 2]),
                                                          ALU.mult)
                                else:
                                    ins = V.tensor_copy(dst[:, q], tile)
                            ins.then_inc(pn_done, 1)
                            if layer == 0 and isinstance(g0, int) and g0 == 0 and k in (3, 6, 9):
                                step(rstd_rows(k // 3))
                        if layer == 1 and lo[4] <= k < lo[5]:
                            h = g - 1
                            ahead = isinstance(h, int) and h < AHEAD
                            if ahead:
                                dve.wait_ge(proj_done[1], NQ * NG + h + 1)
                            else:
                                dve.wait_ge(g_done, h + (1 + NG - 2 * AHEAD))
                            reached(dve, xadd_done, h + (base - 3))
                            bias = bias_all[:, W_G:W_Z].unsqueeze(1).to_broadcast([P, GR, ROW])
                            V.tensor_tensor(sg[(k - 1) % 4].rearrange("p (r m) -> p r m", m=ROW),
                                            PS[:, h if ahead else (k - 1) % 2, :].rearrange("p (r m) -> p r m", m=ROW),
                                            bias, ALU.add).then_inc(gate_bias_added, 1)
                        if lo[2] <= k < lo[3]:
                            h = g - 2
                            dve.wait_ge(z_done, h + (1 + base))
                            dve.wait_ge(sg_done, h + (1 + base))
                            tile = sg[(k + 2) % 4]
                            V.tensor_tensor(tile, PS[:, 6 + k % 2, :], tile, ALU.mult).then_inc(y_done, 1)
                        if layer == 0 and lo[4] <= k < lo[5]:
                            h = g - 5
                            dve.wait_ge(x1t_ready, h + 1)
                            V.bn_stats(REC[:, ds(h * 6, 6)], XT[:, ds(h * GR, GR), :].rearrange("p r n -> p (r n)")
                                       ).then_inc(bn_done, 1)

                third = 5 if layer == 0 else 1
                finish_steps(0, 16, (0, 16, 2, 16, third, 16))
                with dve.Fori(1, NG // 16) as i:
                    finish_steps(i * 16, 16, (0, 16, 0, 16, 0, 16))
                finish_steps(NG, 5, (0, 0, 0, 2, 0, third))

                if layer == 0:
                    dve.wait_ge(bn_done, 2 * NG)
                    dve.wait_ge(raw1_in, 16)
                    group_norm(NT + 3)
                    step(V.tensor_tensor(col(9), col(0), col(6), ALU.mult))
                    step(V.tensor_tensor(col(10), col(9), col(8), ALU.add))
                    step(V.tensor_tensor(col(11), col(6), col(6), ALU.mult))
                    step(V.tensor_tensor(col(11), col(11), col(1), ALU.mult))
                    V.scalar_tensor_tensor(col(11), col(10), col(10), col(11), ALU.mult, ALU.add).then_inc(small_in, 1)
                    answer()
                    step(V.tensor_scalar(T[:, 18:20], PS[:, 7, 4:6], 1.0 / P, None, ALU.mult))
                    step(V.scalar_tensor_tensor(col(7), col(18), col(18), col(19), ALU.mult, ALU.subtract))
                    V.tensor_scalar(col(16), col(7), -1.0, EPS, ALU.mult, ALU.add).then_inc(var_ready, 1)
                    step(rsqrt(col(13), col(16), col(17), NT + 4, col(7)))
                    step(V.tensor_tensor(col(13), col(13), VEC[:, V_AI:V_AI + 1], ALU.mult))
                    step(V.tensor_tensor(col(6), col(6), col(13), ALU.mult))
                    step(V.tensor_tensor(col(8), col(8), col(18), ALU.subtract))
                    step(V.scalar_tensor_tensor(col(8), col(8), col(13), VEC[:, V_BI:V_BI + 1], ALU.mult, ALU.add))
                    final(V.tensor_scalar(EFF[:, 0:W_Z], RAW[:, 0:W_Z], col(6), None, ALU.mult), folded, 2)
                    V.tensor_scalar(shift_all, ones, col(8), None, ALU.mult).then_inc(small_in, 1)
                    answer()
                    step(V.tensor_copy(bias_all[:, 0:BANK], PS[:, 5, :]))
                    step(V.tensor_copy(bias_all[:, W_G:W_Z], PS[:, 6, 0:P]))
                    split3(BROW[:, :], PS[:, 6, P:2 * P], lambda ins: final(ins, biases_ready, 1))

    return nc


def shape_constants():
    k = np.arange(P)
    par, c = k // CH, k % CH
    same = (par[:, None] == par[None, :])
    eye = np.eye(P)
    consts = np.zeros((P, C_N))
    consts[:, C_ID:C_ID + P] = eye
    consts[:, C_GM:C_GM + P] = (c[:, None] // 2 == c[None, :] // 2) / 4
    consts[:, C_ONES:C_ONES + P] = 1
    consts[:, C_E0] = c == 0
    consts[:, C_NE0] = c != 0
    norm = np.zeros((P, L_N))
    norm[:, L_CM:L_CM + P] = eye - same / CH
    norm[:, L_DROP:L_DROP + P] = (eye - (same & (c[:, None] == 0))) * (c[None, :] != 0)
    for part in range(3):
        norm[k, L_SEL + 30 + 32 * part + par] = 1 / CH
    norm[k, L_ECOL + CH * par] = 1
    norm[0, L_BSEL] = 1
    norm[1, L_BSEL + CH] = 1
    spread = np.zeros((P, TG, P))
    for part in range(3):
        for u in range(TG):
            for q in range(2):
                spread[32 * part + 2 * u + q, u, (par == q) & (c != 0)] = 1
    spread[96, :, c == 0] = 1
    ones3 = np.zeros((P, P))
    ones3[[0, 32, 64]] = 1
    return consts, norm, spread.reshape(P, TG * P), ones3


def kernel(**inputs):
    import concourse.bacc as bacc
    from concourse.bass_utils import run_bass_kernel_spmd as run
    import ml_dtypes

    a = {k: np.asarray(v) for k, v in inputs.items()}

    def weights(gate_a, gate_b, lin_a, lin_b, gate_o, lin_o):
        four = np.stack([gate_a, gate_b, lin_a, lin_b], 1).reshape(CH, 2, 2, NQ, CHUNK)
        four = four.transpose(0, 3, 1, 4, 2).reshape(CH, NQ, CH)
        cols = np.concatenate([four, gate_o[:, None], lin_o[:, None]], 1)
        gap = np.zeros_like(cols)
        even = np.stack([cols, gap], 2).reshape(CH, W_N)
        odd = np.stack([gap, cols], 2).reshape(CH, W_N)
        return np.ascontiguousarray(np.concatenate([even, odd], 0))

    def biases(gate_a, gate_b, lin_a, lin_b, gate_o, lin_o):
        four = np.stack([gate_a, gate_b, lin_a, lin_b], 0).reshape(2, 2, NQ, CHUNK)
        cols = np.concatenate([four.transpose(2, 0, 3, 1).reshape(NQ, CH), gate_o[None], lin_o[None]], 0)
        gap = np.zeros_like(cols)
        return np.stack([np.stack([cols, gap], 1).reshape(W_N), np.stack([gap, cols], 1).reshape(W_N)], 0)

    L0, L1 = "L0_conv_", "L1_conv_"
    names0 = [L0 + n for n in ("w_ag", "w_bg", "w_ap", "w_bp", "w_g", "w_z")]
    names1 = [L1 + n for n in ("W_ga", "W_gb", "W_la", "W_lb", "W_go", "W_lo")]
    bias0 = [L0 + n for n in ("b_ag", "b_bg", "b_ap", "b_bp", "b_g", "b_z")]
    bias1 = [L1 + n for n in ("b_ga", "b_gb", "b_la", "b_lb", "b_go", "b_lo")]
    vecs = [np.concatenate([a[L0 + n]] * 2) for n in ("ln_in_w", "ln_in_b", "ln_out_w", "ln_out_b")]
    vecs += [np.repeat(a[L1 + n], P) for n in ("alpha_in", "beta_in", "alpha_o", "beta_o")]
    consts, norm, spread, ones3 = shape_constants()
    arrays = {
        "x": np.ascontiguousarray(a["x"]),
        "mask": np.ascontiguousarray(a[L0 + "mask"]),
        "w0": weights(*(a[n] for n in names0)),
        "w1": weights(*(a[n].T for n in names1)),
        "bias0": biases(*(a[n] for n in bias0)),
        "bias1": biases(*(a[n] for n in bias1)),
        "vecs": np.ascontiguousarray(np.stack(vecs, 1)),
        "consts": consts.astype(np.float32),
        "norm_consts": norm.astype(np.float32),
        "spread": spread.astype(ml_dtypes.bfloat16),
        "ones3": ones3.astype(ml_dtypes.bfloat16),
    }
    nc = bacc.Bacc("TRN2", target_bir_lowering=False, num_devices=1, dynamic_dma_scratch_size=64)
    args = [nc.dram_tensor(n, v.shape, mybir.dt.from_np(v.dtype), kind="ExternalInput").ap()
            for n, v in arrays.items()]
    out = nc.dram_tensor("out", (1, ROWS, COLS, CH), mybir.dt.float32, kind="ExternalOutput").ap()
    build(nc, *args, out)
    r = run(nc, [arrays], core_ids=[0])
    return r.results[0]["out"]
```

```python
import numpy as np
from contextlib import ExitStack

import concourse.bass as bass
from concourse import mybir

ROWS = 256
COLS = 256
CH = 64
P = 128
ROW = 2 * CH
GR = 4
NG = ROWS // GR
BANK = 512
CHUNK = 16
NQ = CH // CHUNK
LOAD_ROWS = 16
LOAD_SLOTS = 4
LG = LOAD_ROWS // GR
BR = 32
BG = BR // GR
NB = ROWS // BR
HR = 16
HG = HR // GR
HS = 4
AHEAD = 4
SPREAD_LAG = 5
TG = 16
NT = NG // TG
QW = 4 * 2 * CHUNK
W_G = NQ * QW
W_Z = W_G + ROW
W_N = W_Z + ROW
EPS = 1e-5
Z_SCALE = 2.0 ** 8
W_TOP = 2.0 ** 13
X_TOP = 2.0 ** 15
SEL = 32 * 2 + 2 + 2 * (TG - 1) + 30

C_ID, C_GM, C_ONES, C_E0, C_NE0, C_N = 0, 128, 256, 384, 385, 386
L_CM, L_DROP, L_SEL, L_ECOL, L_BSEL, L_N = 0, 128, 256, 384, 512, 640
V_LNW, V_LNB, V_OW, V_OB, V_AI, V_BI, V_AO, V_BO, V_N = range(9)


def build(nc, x, mask, w0, w1, bias0, bias1, vecs, consts, norm_consts, spread, ones3, out):
    f32 = mybir.dt.float32
    bf16 = mybir.dt.bfloat16
    f16 = mybir.dt.float16
    i32 = mybir.dt.int32
    ALU = mybir.AluOpType
    ACT = mybir.ActivationFunctionType
    ds = bass.ds

    x_tok = x[0].rearrange("r (p q) c -> p r (q c)", q=2)
    out_tok = out[0].rearrange("r (p q) c -> p r (q c)", q=2)
    p_dram = nc.dram_tensor("p_scratch", [P, CH // 2, 2 * ROWS * 2], f32, kind="Internal").ap()
    p_blocks = p_dram.rearrange("p c (q r e) -> p (c q) (r e)", q=2, e=2)

    ctx = ExitStack()
    with ctx:
        def sb(name, cols, dt=f32):
            return ctx.enter_context(nc.sbuf_tensor(name, [P, cols], dt))

        def sem(name):
            return ctx.enter_context(nc.semaphore(name))

        XT_ALL = sb("XT_ALL", NG * BANK)
        XT = XT_ALL[:, :].rearrange("p (r n) -> p r n", n=P)
        halves = XT_ALL[:, :].bitcast(f16)
        AB = sb("AB", 2 * 2 * CHUNK * ROWS)
        CF = sb("CF", C_N)
        RAW = sb("RAW", W_N)
        EFF = sb("EFF", W_N)
        BROW = sb("BROW", ROW, bf16)
        ONES3 = sb("ONES3", P, bf16)
        MS = sb("MS", 2 * BANK)
        S1 = sb("S1", BANK)
        WK = sb("WK", 7 * BANK)
        REC = sb("REC", 6 * NG)
        rows_tmp = sb("rows_tmp", 2 * ROWS // 4)
        VEC = sb("VEC", V_N)
        T = sb("T", 32)
        unscale = sb("unscale", P, bf16)
        table_tmp = sb("table_tmp", 12)
        PS = ctx.enter_context(nc.psum_tensor("PS", [P, 8, BANK], f32))

        w_hi, w_lo = (EFF[:, 0:W_Z].bitcast(f16)[:, i * W_Z:(i + 1) * W_Z] for i in range(2))

        def half(g, i):
            return halves[:, ds(g * (2 * BANK) + i * BANK, BANK)]

        ident = CF[:, C_ID:C_ID + P]
        group_mean = CF[:, C_GM:C_GM + P]
        ones = CF[:, C_ONES:C_ONES + P]

        bias_all = RAW[:, 0:W_Z]
        shift_all = EFF[:, W_Z:W_N]

        xs = AB[:, 0:LOAD_SLOTS * LOAD_ROWS * ROW].rearrange("p (s r m) -> p s r m", s=LOAD_SLOTS, m=ROW)
        at = LOAD_SLOTS * LOAD_ROWS * ROW

        def part(n):
            nonlocal at
            at += n
            return AB[:, at - n:at]

        zn = xs.rearrange("p s r m -> p (s r m)")[:, 0:8 * BANK].rearrange("p (s n) -> p s n", s=8)

        NCF = part(L_N)
        maskn = part(2 * COLS)
        brow0 = part(W_N)
        spread_sb = part(TG * P // 2).bitcast(bf16)
        sq = part(2 * BANK).rearrange("p (s n) -> p s n", s=2)
        ve, sd, rt, tmp = (part(BANK) for _ in range(4))
        parts3 = part(BANK // 2).bitcast(bf16)
        cs = part(P)
        wW = part(W_N)
        lnb_col = part(P)
        lnb_all = part(P)
        diag = part(P)
        out_sq = part(P)
        assert at <= 2 * 2 * CHUNK * ROWS
        ab = AB[:, :].rearrange("p (q k r) -> p q k r", q=2, r=ROWS)
        ptb = AB[:, 0:2 * CH * BR * 2].rearrange("p (s m n) -> p s m n", s=2, n=2 * BR)
        xb = AB[:, 2 * CH * BR * 2:4 * CH * BR * 2].rearrange("p (s r m) -> p s r m", s=HS, m=ROW)

        sig = WK[:, 0:4 * 256].rearrange("p (s t k) -> p s t k", s=4, k=2 * CHUNK)
        st = WK[:, 1024:1024 + 4 * BANK].rearrange("p (s n e) -> p s n e", s=2, e=2)
        sqp = WK[:, 6 * BANK:7 * BANK]
        biased = [WK[:, 0:BANK], WK[:, BANK:2 * BANK], WK[:, 6 * BANK:7 * BANK], S1[:, :]]
        pn = WK[:, 0:2 * BANK].rearrange("p (s r m) -> p s r m", s=2, m=ROW)
        pt = WK[:, 2 * BANK:4 * BANK].rearrange("p (s n) -> p s n", s=2)
        sg = [WK[:, 4 * BANK:5 * BANK], WK[:, 5 * BANK:6 * BANK], MS[:, 0:BANK], MS[:, BANK:2 * BANK]]
        maskT = MS[:, 0:BANK].rearrange("p (q r) -> p q r", q=2)
        S2 = MS[:, BANK:2 * BANK]
        brow1 = MS[:, 0:W_N]
        spare, spare_bf = rows_tmp[:, :], WK[:, 2 * BANK:2 * BANK + P // 2].bitcast(bf16)
        rstd2 = S1[:, :].rearrange("p (q r) -> p q r", q=2)

        ident_in = sem("ident_in")
        mask_in = sem("mask_in")
        consts_in = sem("consts_in")
        raw1_in = sem("raw1_in")
        brow1_in = sem("brow1_in")
        xs_in = [sem(f"xs_in{s}") for s in range(LOAD_SLOTS)]
        tr_done = sem("tr_done")
        xt_ready = sem("xt_ready")
        bn_done = sem("bn_done")
        mask_tr = sem("mask_tr")
        mask_ready = sem("mask_ready")
        dve_step = sem("dve_step")
        dve_chain = sem("dve_chain")
        s1_done = sem("s1_done")
        small_in = sem("small_in")
        small_out = sem("small_out")
        var_ready = sem("var_ready")
        std_ready = sem("std_ready")
        norm_ready = sem("norm_ready")
        folded = sem("folded")
        hi_done = sem("hi_done")
        lo_done = sem("lo_done")
        lo_done_v = sem("lo_done_v")
        bound_ready = sem("bound_ready")
        bound_root = sem("bound_root")
        x1split_done = sem("x1split_done")
        biases_ready = sem("biases_ready")
        weights_ready = sem("weights_ready")
        mm1_done = sem("mm1_done")
        zc_done = sem("zc_done")
        sq_ready = sem("sq_ready")
        mm2_done = sem("mm2_done")
        rb_ready = sem("rb_ready")
        bc_done = sem("bc_done")
        zn_done = sem("zn_done")
        proj_done = [sem(f"proj_done{layer}") for layer in range(2)]
        sig_done = sem("sig_done")
        msk_done = sem("msk_done")
        bias_added = sem("bias_added")
        gate_bias_added = sem("gate_bias_added")
        prod_done = [sem(f"prod_done{layer}") for layer in range(2)]
        ein_done = sem("ein_done")
        st_ready = sem("st_ready")
        sqp_ready = sem("sqp_ready")
        acc_done = sem("acc_done")
        p_stored = [sem(f"p_stored{s}") for s in range(2)]
        p_in = [sem(f"p_in{s}") for s in range(2)]
        xb_in = [sem(f"xb_in{s}") for s in range(HS)]
        xb_stored = [sem(f"xb_stored{s}") for s in range(HS)]
        pn_done = sem("pn_done")
        pn_done_p = sem("pn_done_p")
        rstd_ready = sem("rstd_ready")
        tb_done = sem("tb_done")
        pt_ready = sem("pt_ready")
        g_done = sem("g_done")
        sg_done = sem("sg_done")
        z_done = sem("z_done")
        y_done = sem("y_done")
        xadd_done = sem("xadd_done")
        x1tr_done = sem("x1tr_done")
        x1back_done = sem("x1back_done")
        x1t_ready = sem("x1t_ready")

        N_CONSTS = 6

        block = ctx.enter_context(nc.Block())

        def rounds(eng, body, n, peeled, last=None, done=0):
            for i in range(done, peeled):
                body(i)
            with eng.Fori(peeled, n if last is None else n - 1) as i:
                body(i)
            if last is not None:
                last(n - 1)

        def new_x_bank(g):
            return g % 2 + (0 if isinstance(g, int) and g >= NG - 2 else 2)

        LOWS_V = [u for u in range(TG) if u % 3 == 1]

        def low_count(u):
            return NG - TG + sum(v not in LOWS_V for v in range(u + 1))

        def reached(eng, semaphore, value):
            if not isinstance(value, int) or value > 0:
                eng.wait_ge(semaphore, value)

        @block.sync
        def _(sp):
            def load_x(row, s):
                for h in range(2):
                    sp.dma_start(xs[:, s, h * LOAD_ROWS // 2:(h + 1) * LOAD_ROWS // 2, :],
                                 x_tok[:, ds(row + h * LOAD_ROWS // 2, LOAD_ROWS // 2), :]).then_inc(xs_in[s], 16)

            sp.dma_start(CF[:, :], consts).then_inc(ident_in, 16)
            load_x(0 * LOAD_ROWS, 0)
            load_x(1 * LOAD_ROWS, 1)
            sp.dma_start(maskn.rearrange("p (h c) -> p h c", h=2),
                         mask[0].rearrange("(h p) c -> p h c", h=2)).then_inc(mask_in, 16)
            load_x(2 * LOAD_ROWS, 2)
            load_x(3 * LOAD_ROWS, 3)
            with sp.Fori(1, ROWS // LOAD_ROWS // LOAD_SLOTS) as t4:
                for s in range(LOAD_SLOTS):
                    row = sp.snap(t4 * (LOAD_SLOTS * LOAD_ROWS) + s * LOAD_ROWS)
                    sp.wait_ge(tr_done, t4 * (LG * LOAD_SLOTS) + LG * (s + 1 - LOAD_SLOTS))
                    load_x(row, s)
            for dst, src in ((NCF, norm_consts), (VEC[:, :], vecs), (RAW[:, :], w0),
                             (brow0[0:2, :], bias0), (spread_sb, spread), (ONES3[:, :], ones3)):
                sp.dma_start(dst, src).then_inc(consts_in, 16)
            for layer in range(2):
                if layer == 0:
                    sp.wait_ge(small_out, 4)
                    sp.dma_start(RAW[:, :], w1).then_inc(raw1_in, 16)
                def store_pair(q, pair):
                    at_pair = q * (CHUNK // 2) + pair
                    if not isinstance(q, int):
                        at_pair = sp.snap(at_pair)
                    sp.wait_ge(st_ready, q * CHUNK + (2 * pair + 2 + CH * layer))
                    sp.dma_start(p_dram[:, ds(at_pair, 1), :],
                                 st[:, pair % 2].rearrange("p n e -> p (n e)").unsqueeze(1)
                                 ).then_inc(p_stored[pair % 2], 16)

                def load_p(row, s):
                    for h in range(4):
                        sp.dma_start(ptb[:, s, h * CH // 4:(h + 1) * CH // 4, :],
                                     p_blocks[:, h * CH // 4:(h + 1) * CH // 4, ds(row * 2, 2 * BR)]
                                     ).then_inc(p_in[s], 16)

                def load_rows(row, s):
                    for h in range(2):
                        sp.dma_start(xb[:, s, h * HR // 2:(h + 1) * HR // 2, :],
                                     x_tok[:, ds(row + h * HR // 2, HR // 2), :]).then_inc(xb_in[s], 16)

                def store_rows(row, s):
                    sp.dma_start(out_tok[:, ds(row, HR), :], xb[:, s]).then_inc(xb_stored[s], 16)

                with sp.Fori(0, NQ - 1) as q:
                    for pair in range(CHUNK // 2):
                        store_pair(q, pair)
                first_pieces = {0: (0, 16), 2: (16, 36), 4: (36, 56)}
                for pair in range(CHUNK // 2):
                    store_pair(NQ - 1, pair)
                    if pair in first_pieces:
                        lo, hi = first_pieces[pair]
                        stored = (CH - CHUNK + 2 * max((hi - CH + CHUNK) // 2, 0)) // 4
                        for s in range(2):
                            sp.wait_ge(p_stored[s], 16 * (CH // 4 * layer + stored))
                        sp.wait_ge(ein_done, CH * layer + CH - CHUNK + hi // 8 + 1)
                        sp.dma_start(ptb[:, 0, lo:hi, :], p_blocks[:, lo:hi, 0:2 * BR]).then_inc(p_in[0], 16)
                for s in range(2):
                    sp.wait_ge(p_stored[s], 16 * (CH // 4) * (layer + 1))
                sp.dma_start(ptb[:, 0, 56:CH, :], p_blocks[:, 56:CH, 0:2 * BR]).then_inc(p_in[0], 16)
                if layer == 0:
                    load_rows(0, 0)
                    load_rows(HR, 1)
                load_p(BR, 1)
                if layer == 0:
                    load_rows(2 * HR, 2)
                    load_rows(3 * HR, 3)

                with sp.Fori(0, NB // 2 - 1) as b2:
                    for s in range(2):
                        for h in range(2):
                            slot = 2 * s + h
                            row = sp.snap(b2 * (2 * BR) + (slot * HR + (HS * HR if layer == 0 else 0)))
                            p_row = sp.snap(b2 * (2 * BR) + (s * BR + 2 * BR))
                            groups = sp.snap(b2 * (2 * BG) + ((slot + 1) * HG + NG * layer))
                            tiles = sp.snap(b2 * (2 * BG) + ((s + 1) * BG + NG * layer))
                            if layer == 0:
                                sp.wait_ge(x1tr_done, groups)
                                load_rows(row, slot)
                            else:
                                sp.wait_ge(xadd_done, groups)
                                store_rows(row, slot)
                            if h == 0:
                                sp.wait_ge(tb_done, tiles)
                                load_p(p_row, s)
                if layer == 0:
                    sp.wait_ge(xadd_done, NG)
                    sp.dma_start(brow1[0:2, :], bias1).then_inc(brow1_in, 16)
                else:
                    for slot in range(HS):
                        sp.wait_ge(xadd_done, 2 * NG - (HS - 1 - slot) * HG)
                        store_rows(ROWS - (HS - slot) * HR, slot)
                    for slot in range(HS):
                        sp.wait_ge(xb_stored[slot], 16 * (NB // 2))

        @block.tensor
        def _(pe):
            def mm(dst, lhsT, rhs, start=True, stop=True):
                return nc.tensor.matmul(dst, lhsT, rhs, start=start, stop=stop)

            pe.wait_ge(ident_in, 16)

            def transpose_loads(t4):
                for s in range(LOAD_SLOTS):
                    for u in range(LG):
                        g = s * LG + u
                        if u == 0:
                            pe.wait_ge(xs_in[s], t4 * 32 + 32)
                        reached(pe, xt_ready, t4 * (LG * LOAD_SLOTS) + (g - 3))
                        for r in range(GR):
                            last = nc.tensor.transpose(PS[:, g % 4, r * P:(r + 1) * P], xs[:, s, u * GR + r, :], ident)
                        last.then_inc(tr_done, 1)

            transpose_loads(0)
            pe.wait_ge(mask_in, 16)
            for q in range(2):
                for h in range(2):
                    src = maskn.rearrange("p (h c q) -> p h q c", h=2, q=2)[:, h, q]
                    last = nc.tensor.transpose(PS[:, 7, (2 * q + h) * P:(2 * q + h + 1) * P], src, ident)
            last.then_inc(mask_tr, 1)
            with pe.Fori(1, ROWS // LOAD_ROWS // LOAD_SLOTS) as t4:
                transpose_loads(t4)

            smalls = [0]

            def small(pairs):
                smalls[0] += 1
                pe.wait_ge(small_in, smalls[0])
                for args in pairs:
                    last = mm(*args)
                last.then_inc(small_out, 1)

            pe.wait_ge(mask_ready, 1)
            small([(PS[:, 7, 0:1], group_mean, T[:, 0:1])])
            small([(PS[:, 7, 2:3], group_mean, T[:, 3:4])])
            pe.wait_ge(consts_in, 16 * N_CONSTS)
            cm, drop = NCF[:, L_CM:L_CM + P], NCF[:, L_DROP:L_DROP + P]
            bsel = NCF[0:2, L_BSEL:L_BSEL + P]
            small([(PS[:, 7, 4:5], cm, T[:, 8:9])])

            def fold_weights():
                small([(PS[:, 5, :], drop, wW[:, 0:BANK], True, False),
                       (PS[:, 5, :], lnb_col, RAW[:, 0:BANK], False, False),
                       (PS[:, 5, :], bsel, brow0[0:2, 0:BANK], False, True),
                       (PS[:, 6, 0:P], drop, wW[:, W_G:W_Z], True, False),
                       (PS[:, 6, 0:P], lnb_col, RAW[:, W_G:W_Z], False, False),
                       (PS[:, 6, 0:P], bsel, brow0[0:2, W_G:W_Z], False, True),
                       (PS[:, 6, P:2 * P], cm, wW[:, W_Z:W_N]),
                       (PS[:, 6, 2 * P:3 * P], lnb_all, RAW[:, W_Z:W_N], True, False),
                       (PS[:, 6, 2 * P:3 * P], ones[0:2, :], brow0[0:2, W_Z:W_N], False, True),
                       (PS[:, 6, 3 * P:3 * P + 1], RAW[:, W_Z:W_N], VEC[:, V_OB:V_OB + 1], True, False),
                       (PS[:, 6, 3 * P:3 * P + 1], brow0[0:2, W_Z:W_N], ones[0:2, 0:1], False, True)])

            def spread_rstd(t, u):
                if u == 0:
                    pe.wait_ge(rb_ready, t + 1)
                reached(pe, zn_done, t * TG + max(u - 1, 0))
                mm(PS[:, 5 + u % 2, :], spread_sb[:, u * P:(u + 1) * P], parts3).then_inc(bc_done, 1)

            def round_(t):
                spread = 0
                for u in range(TG + 1):
                    if u < TG:
                        reached(pe, sq_ready, t * TG + (u - 3))
                        mm(PS[:, u % 4, :], cs, XT[:, ds(t * (TG * GR) + u * GR, GR), :].rearrange("p r n -> p (r n)")
                           ).then_inc(mm1_done, 1)
                    if u >= 1:
                        v = u - 1
                        pe.wait_ge(sq_ready, t * TG + (v + 1))
                        if v == 0:
                            reached(pe, var_ready, t + 1)
                        s0 = L_SEL + 30 - 2 * v
                        mm(PS[0:96, 4, :], NCF[:, s0:s0 + 96], sq[:, v % 2], v == 0, v == TG - 1).then_inc(mm2_done, 1)
                    if isinstance(t, int) and t == 0:
                        if u == SPREAD_LAG:
                            fold_weights()
                        if u == 2 * SPREAD_LAG:
                            small([(PS[:, 7, P:2 * P], ones, diag),
                                   (PS[:, 7, 2 * P:2 * P + 1], out_sq, ones[:, 0:1])])
                    elif SPREAD_LAG <= u < TG:
                        for _ in range(1 if (u - SPREAD_LAG) % 2 or u == TG - 1 else 2):
                            spread_rstd(t - 1, spread)
                            spread += 1
                assert spread in (0, TG)

            rounds(pe, round_, NT, 2)
            for layer in range(2):
                free = sqp_ready if layer == 0 else st_ready

                def rows_times(bank, g, r, column):
                    dst = bank[:, r * QW:(r + 1) * QW]
                    hi, lo = (half(g, i)[:, r * P:(r + 1) * P] for i in range(2))
                    mm(dst, hi, w_hi[:, ds(column, QW)], True, False)
                    mm(dst, hi, w_lo[:, ds(column, QW)], False, False)
                    return mm(dst, lo, w_hi[:, ds(column, QW)], False, True)

                def project(q, g):
                    bank = PS[:, g % 8, :]
                    if 4 <= g < 8:
                        if not isinstance(q, int) or q > 0:
                            pe.wait_ge(free, q * CHUNK + (g - 7 + CH * layer))
                    else:
                        reached(pe, prod_done[0] if layer == 0 else bias_added, q * NG + (g - 7))
                    for r in range(GR):
                        last = rows_times(bank, g, r, q * QW)
                    last.then_inc(proj_done[layer], 1)

                def chunk(q):
                    for g in range(AHEAD, NG):
                        project(q, g)
                    for g in range(AHEAD):
                        project(q + 1, g)
                    pe.wait_ge(prod_done[layer], q * NG + NG)
                    for c in range(CHUNK):
                        reached(pe, free, q * CHUNK + (max(c - 3, 0) + CH * layer))
                        for jq in range(2):
                            for kq in range(2):
                                last = mm(PS[:, 4 + c % 4, jq * ROWS:(jq + 1) * ROWS],
                                          ab[:, kq, 2 * c + 1, jq::2], ab[:, kq, 2 * c, :], kq == 0, kq == 1)
                        last.then_inc(ein_done, 1)

                if layer == 1:
                    small([(PS[:, 7, P:2 * P], ones, diag)])
                    small([(PS[:, 5, :], shift_all, RAW[:, 0:BANK], False, True),
                           (PS[:, 6, 0:P], shift_all, RAW[:, W_G:W_Z], False, True)])
                    pe.wait_ge(x1split_done, NG)
                pe.wait_ge(folded, layer + 1)
                if layer == 0:
                    pe.wait_ge(lo_done, AHEAD)
                for g in range(AHEAD):
                    project(0, g)
                if layer == 0:
                    for u in range(TG):
                        spread_rstd(NT - 1, u)
                    pe.wait_ge(lo_done, low_count(TG - 1))
                    pe.wait_ge(lo_done_v, len(LOWS_V))
                else:
                    pe.wait_ge(biases_ready, 1)
                rounds(pe, chunk, NQ, 1 - layer)

                if layer == 1:
                    small([(PS[:, 7, 0:1], ones, T[:, 0:1])])
                    small([(PS[:, 7, 2:3], ones, T[:, 3:4])])
                w_out = (EFF if layer == 0 else RAW)[:, W_Z:W_N]
                base = NG * layer
                pe.wait_ge(free, CH * (layer + 1) if layer == 1 else CH)
                for step in range(NG + 3):
                    g = step
                    if g < NG:
                        pe.wait_ge(pn_done, base + g + 1)
                        if layer == 0:
                            pe.wait_ge(pn_done_p, g + 1)
                        reached(pe, pt_ready, base + g - 1)
                        for r in range(GR):
                            last = nc.tensor.transpose(PS[:, 4 + g % 2, r * P:(r + 1) * P], pn[:, g % 2, r, :], ident)
                        last.then_inc(tb_done, 1)
                    if AHEAD <= g < NG:
                        pe.wait_ge(sg_done if layer == 0 else gate_bias_added, g - 1)
                        for r in range(GR):
                            last = rows_times(PS[:, g % 2, :], g, r, W_G)
                        last.then_inc(g_done, 1)
                    g = step - 1
                    if 0 <= g < NG:
                        pe.wait_ge(pt_ready, base + g + 1)
                        reached(pe, y_done, base + g - 1)
                        bank = PS[:, 6 + g % 2, :]
                        mm(bank, ONES3[:, :], BROW[:, :].unsqueeze(1).to_broadcast([P, GR, ROW]), True, False)
                        for r in range(GR):
                            last = mm(bank[:, r * P:(r + 1) * P], pt[:, g % 2, r * P:(r + 1) * P], w_out,
                                      False, r == GR - 1)
                        last.then_inc(z_done, 1)
                    g = step - 3
                    if layer == 0 and 0 <= g < NG:
                        pe.wait_ge(xadd_done, g + 1)
                        if g < 2:
                            pe.wait_ge(sg_done, g + 3)
                        if g < NG - 2:
                            reached(pe, x1split_done, g - 1)
                        else:
                            pe.wait_ge(sg_done, NG)
                        for r in range(GR):
                            row = g * GR + r
                            last = nc.tensor.transpose(PS[:, new_x_bank(g), r * P:(r + 1) * P],
                                                       xb[:, row // HR % HS, row % HR, :], ident)
                        last.then_inc(x1tr_done, 1)
                    g = step - 1
                    if layer == 1 and 0 <= g < NG:
                        if g < 2:
                            pe.wait_ge(gate_bias_added, g + 3)
                        else:
                            pe.wait_ge(xadd_done, base + g - 1)
                        for r in range(GR):
                            dst = PS[:, 2 + g % 2, r * P:(r + 1) * P]
                            mm(dst, half(g, 0)[:, r * P:(r + 1) * P], unscale[:, :], True, False)
                            last = mm(dst, half(g, 1)[:, r * P:(r + 1) * P], unscale[:, :], False, True)
                        last.then_inc(x1back_done, 1)

                if layer == 0:
                    pe.wait_ge(brow1_in, 16)
                    pe.wait_ge(y_done, NG)
                    pe.wait_ge(pt_ready, NG)
                    mm(PS[:, 5, :], ones[0:2, :], brow1[0:2, 0:BANK], True, False)
                    mm(PS[:, 6, P:2 * P], ones[0:2, :], brow1[0:2, W_Z:W_N])
                    mm(PS[:, 6, 0:P], ones[0:2, :], brow1[0:2, W_G:W_Z], True, False)
                    small([(PS[:, 7, 0:1], group_mean, T[:, 0:1])])
                    small([(PS[:, 7, 2:3], group_mean, T[:, 3:4])])
                    small([(PS[:, 7, 4:6], ones, T[:, 10:12])])

        @block.scalar
        def _(act):
            def transposed(t4):
                for g in range(LG * LOAD_SLOTS):
                    n = t4 * (LG * LOAD_SLOTS) + g
                    act.wait_ge(tr_done, n + 1)
                    nc.scalar.activation(XT[:, ds(n * GR, GR), :].rearrange("p r n -> p (r n)"), PS[:, g % 4, :],
                                         ACT.Copy).then_inc(xt_ready, 1)

            transposed(0)
            act.wait_ge(mask_tr, 1)
            nc.scalar.activation(maskT.rearrange("p q r -> p (q r)"), PS[:, 7, :], ACT.Copy).then_inc(mask_ready, 1)
            with act.Fori(1, ROWS // LOAD_ROWS // LOAD_SLOTS) as t4:
                transposed(t4)

            tables = [0]

            def load_table(function):
                nc.scalar.activation(table_tmp[:, tables[0]:tables[0] + 1], CF[:, C_ONES:C_ONES + 1], function)
                tables[0] += 1

            def root(n, dst, src, ahead=True):
                if ahead:
                    load_table(ACT.Sqrt)
                act.wait_ge(var_ready, n)
                nc.scalar.activation(dst, src, ACT.Sqrt).then_inc(std_ready, 1)

            root(1, T[:, 5:6], T[:, 4:5])
            act.wait_ge(norm_ready, 1)

            def centred(t, last=False):
                for u in range(TG):
                    n = t * TG + u
                    act.wait_ge(mm1_done, n + 1)
                    nc.scalar.activation(XT[:, ds(n * GR, GR), :].rearrange("p r n -> p (r n)"), PS[:, u % 4, :],
                                         ACT.Identity, bias=T[:, 15:16], scale=CF[:, C_NE0:C_NE0 + 1]
                                         ).then_inc(zc_done, 1)
                    reached(act, mm2_done, n - 1)
                    nc.scalar.activation(sq[:, u % 2], PS[:, u % 4, :], ACT.Square, bias=T[:, 14:15]
                                         ).then_inc(sq_ready, 1)
                if isinstance(t, int) and t == 0:
                    act.wait_ge(bound_ready, 1)
                    nc.scalar.activation(T[:, 23:24], T[:, 24:25], ACT.Sqrt).then_inc(bound_root, 1)
                root(t + 2, sd[0:96, :], ve[0:96, :], ahead=last)

            rounds(act, centred, NT, 1, lambda t: centred(t, last=True))
            load_table(ACT.Sigmoid)
            for u in range(TG):
                n = NG - TG + u
                act.wait_ge(zn_done, n + 1)
                nc.scalar.activation(half(n, 0), zn[:, u % 8], ACT.Copy).then_inc(hi_done, 1)

            for layer in range(2):
                base = NQ * NG * layer

                def gates(q, g0, us):
                    for u in us:
                        n = q * NG + (g0 + u)
                        if layer == 0:
                            act.wait_ge(proj_done[0], n + 1)
                            reached(act, prod_done[0], n - 3)
                            nc.scalar.activation(
                                sig[:, u % 4],
                                PS[:, u, :].rearrange("p (t k) -> p t k", k=4 * CHUNK)[:, :, 0:2 * CHUNK],
                                ACT.Sigmoid, scale=T[:, 22:23]).then_inc(sig_done, 1)
                        else:
                            act.wait_ge(bias_added, n + 1)
                            tile = biased[u % 4].rearrange("p (t k) -> p t k", k=4 * CHUNK)[:, :, 0:2 * CHUNK]
                            nc.scalar.activation(tile, tile, ACT.Sigmoid).then_inc(sig_done, 1)

                def chunk(q, last=False):
                    gates(q, 0, range(AHEAD, 8))
                    with act.Fori(1, NG // 8) as g8:
                        gates(q, g8 * 8, range(8))
                    if not last:
                        gates(q + 1, 0, range(AHEAD))
                    for c in range(CHUNK):
                        s = (c // 2) % 2
                        act.wait_ge(ein_done, q * CHUNK + (c + 1 + CH * layer))
                        if c % 2 == 0:
                            reached(act, p_stored[s], q * (16 * CHUNK // 4) + 16 * (c // 4 + CH // 4 * layer))
                            reached(act, acc_done, q * CHUNK + (max(c - 2, 0) + CH * layer))
                        nc.scalar.activation(st[:, s, :, c % 2], PS[:, 4 + c % 4, :], ACT.Copy).then_inc(st_ready, 1)
                        if layer == 0:
                            reached(act, acc_done, q * CHUNK + c)
                            nc.scalar.activation(sqp, PS[:, 4 + c % 4, :], ACT.Square).then_inc(sqp_ready, 1)

                gates(0, 0, range(AHEAD))
                rounds(act, chunk, NQ, 1 - layer, lambda q: chunk(q, last=True))

                base = NG * layer
                if layer == 0:
                    root(NT + 2, S1[:, :], sqp)
                    load_table(ACT.Sigmoid)
                else:
                    root(NT + 5, T[:, 5:6], T[:, 4:5])
                    load_table(ACT.Sigmoid)
                act.wait_ge(weights_ready, layer + 1)
                for s in range(2):
                    act.wait_ge(p_stored[s], 16 * (CH // 4) * (layer + 1))

                def finish_steps(g0, n_steps, lo):
                    for k in range(n_steps):
                        g = g0 + k
                        if lo[0] <= k < lo[1]:
                            act.wait_ge(tb_done, g + (1 + base))
                            reached(act, z_done, g + (base - 1))
                            if layer == 1:
                                nc.scalar.activation(pt[:, k % 2], PS[:, 4 + k % 2, :], ACT.Identity,
                                                     bias=T[:, 8:9], scale=T[:, 6:7]).then_inc(pt_ready, 1)
                            else:
                                nc.scalar.activation(pt[:, k % 2], PS[:, 4 + k % 2, :], ACT.Copy
                                                     ).then_inc(pt_ready, 1)
                                ahead = isinstance(g, int) and g < AHEAD
                                if ahead:
                                    act.wait_ge(proj_done[0], NQ * NG + g + 1)
                                else:
                                    act.wait_ge(g_done, g - (AHEAD - 1))
                                reached(act, xadd_done, g - 3)
                                nc.scalar.activation(sg[k % 4], PS[:, k if ahead else k % 2, :], ACT.Sigmoid,
                                                     scale=T[:, 22:23]).then_inc(sg_done, 1)
                        if layer == 1 and lo[2] <= k < lo[3]:
                            act.wait_ge(gate_bias_added, g)
                            tile = sg[(k - 1) % 4]
                            nc.scalar.activation(tile, tile, ACT.Sigmoid).then_inc(sg_done, 1)
                        if layer == 0 and lo[2] <= k < lo[3]:
                            h = g - 4
                            act.wait_ge(x1tr_done, h + 1)
                            act.wait_ge(bn_done, h + (1 + NG))
                            bank = new_x_bank(h) if isinstance(h, int) else 2 + k % 2
                            nc.scalar.activation(half(h, 0), PS[:, bank, :], ACT.Identity, scale=T[:, 25:26]
                                                 ).then_inc(x1t_ready, 1)

                first = 4 if layer == 0 else 1
                finish_steps(0, 16, (0, 16, first, 16))
                with act.Fori(1, NG // 16) as i:
                    finish_steps(i * 16, 16, (0, 16, 0, 16))
                finish_steps(NG, first, (0, 0, 0, first))
                if layer == 0:
                    root(NT + 3, T[:, 5:6], T[:, 4:5])
                    root(NT + 4, T[:, 17:18], T[:, 16:17], ahead=False)
                    load_table(ACT.Sigmoid)

        @block.gpsimd
        def _(pool):
            def low(n, u):
                pool.wait_ge(hi_done, n + 1)
                nc.gpsimd.tensor_tensor(half(n, 1), zn[:, u % 8], half(n, 0), ALU.subtract).then_inc(lo_done, 1)

            with pool.Fori(0, (NG - TG) // 8) as t:
                for u in range(8):
                    low(t * 8 + u, u)
            for u in range(TG):
                if u not in LOWS_V:
                    low(NG - TG + u, u)

            with pool.Fori(0, NQ) as q:
                with pool.Fori(0, NG // 8) as g8:
                    for u in range(8):
                        pool.wait_ge(sig_done, q * NG + (g8 * 8 + (u + 1)))
                        rows = maskT[:, :, ds(g8 * (8 * GR) + u * GR, GR)].rearrange("p q r -> p r q")
                        tile = sig[:, u % 4].rearrange("p (r q) k -> p r q k", q=2)
                        nc.gpsimd.tensor_tensor(tile, tile, rows.unsqueeze(3).to_broadcast([P, GR, 2, 2 * CHUNK]),
                                                ALU.mult).then_inc(msk_done, 1)
            pool.wait_ge(weights_ready, 1)

            def finish_steps(g0, n_steps, lo):
                for k in range(n_steps):
                    g = g0 + k
                    if lo[0] <= k < lo[1]:
                        s, u = (k // BG) % 2, k % BG
                        if u == 0:
                            pool.wait_ge(p_in[s], g0 * 4 + 64)
                        if k == 0:
                            reached(pool, rstd_ready, g0 // 16 if isinstance(g0, int) else quarter[0])
                        reached(pool, tb_done, g - 1)
                        src = ptb[:, s].rearrange("p (c q) (r e) -> p q c r e", q=2, e=2)
                        dst = pn[:, k % 2].rearrange("p r (q c e) -> p q c r e", q=2, e=2)
                        rs = rstd2[:, 1, ds(g * GR, GR)].unsqueeze(1).unsqueeze(3)
                        nc.gpsimd.tensor_tensor(dst[:, 1], src[:, 1, :, u * GR:(u + 1) * GR, :],
                                                rs.to_broadcast([P, CH // 2, GR, 2]), ALU.mult).then_inc(pn_done_p, 1)
                    if lo[2] <= k < lo[3]:
                        h, slot, u = g - 3, (k - 3) // HG % HS, (k - 3) % HG
                        if u == 0:
                            pool.wait_ge(xb_in[slot], g0 * 2 + (32 if k >= 3 else 0))
                        pool.wait_ge(y_done, h + 1)
                        rows = xb[:, slot, u * GR:(u + 1) * GR, :].rearrange("p r m -> p (r m)")
                        nc.gpsimd.tensor_tensor(rows, rows, sg[(k + 1) % 4], ALU.add).then_inc(xadd_done, 1)

            quarter = [0]
            finish_steps(0, 16, (0, 16, 3, 16))
            with pool.Fori(1, NG // 16) as i:
                quarter[0] = i
                finish_steps(i * 16, 16, (0, 16, 0, 16))
            finish_steps(NG, 3, (0, 0, 0, 3))

            def product(q, g0, u):
                pool.wait_ge(sig_done, q * NG + (g0 + (u + 1 + NQ * NG)))
                v = biased[u % 4].rearrange("p (r q k) -> p r q k", q=2, k=4 * CHUNK)
                rows = ab[:, :, :, ds(g0 * GR + u * GR, GR)].rearrange("p q k r -> p r q k")
                nc.gpsimd.tensor_tensor(rows, v[:, :, :, 2 * CHUNK:4 * CHUNK], v[:, :, :, 0:2 * CHUNK], ALU.mult
                                        ).then_inc(prod_done[1], 1)

            with pool.Fori(0, NQ) as q:
                pool.wait_ge(ein_done, q * CHUNK + CH)
                for u in range(4):
                    product(q, 0, u)
                with pool.Fori(0, (NG - 4) // 12) as i:
                    for u in range(12):
                        product(q, i * 12 + 4, u)

        @block.vector
        def _(dve):
            steps = [0]
            counts = {"small": 0}

            def step(ins):
                steps[0] += 1
                ins.then_inc(dve_step, 1)
                dve.wait_ge(dve_step, steps[0])

            def answer():
                counts["small"] += 1
                dve.wait_ge(small_out, counts["small"])

            def col(i):
                return T[:, i:i + 1]

            V = nc.vector

            def final(ins, semaphore, value):
                ins.then_inc(semaphore, 1)
                dve.wait_ge(semaphore, value)

            def rsqrt(dst, var, std, n, tmp_):
                dve.wait_ge(std_ready, n)
                step(V.reciprocal(dst, std))
                step(V.scalar_tensor_tensor(tmp_, dst, -0.5, dst, ALU.mult, ALU.mult))
                step(V.tensor_tensor(tmp_, tmp_, var, ALU.mult))
                return V.scalar_tensor_tensor(dst, tmp_, 1.5, dst, ALU.add, ALU.mult)

            def group_norm(n, meanwhile=lambda: None):
                V.bn_aggr(T[:, 0:2], REC[:, :]).then_inc(small_in, 1)
                meanwhile()
                answer()
                step(V.tensor_copy(col(2), PS[:, 7, 0:1]))
                step(V.tensor_tensor(col(7), col(0), col(2), ALU.subtract))
                V.scalar_tensor_tensor(col(3), col(7), col(7), col(1), ALU.mult, ALU.add).then_inc(small_in, 1)
                answer()
                V.tensor_scalar(col(4), PS[:, 7, 2:3], EPS, None, ALU.add).then_inc(var_ready, 1)
                step(rsqrt(col(6), col(4), col(5), n, col(7)))
                step(V.scalar_tensor_tensor(col(8), col(2), -1.0, col(6), ALU.mult, ALU.mult))

            def largest_weight(meanwhile=lambda: None):
                step(V.tensor_reduce(col(20), wW[:, 0:W_Z], mybir.AxisListType.X, ALU.max, apply_absolute_value=True))
                V.tensor_scalar(diag, ident, col(20), None, ALU.mult).then_inc(small_in, 1)
                meanwhile()
                answer()
                step(V.tensor_reduce(col(20), PS[:, 7, P:2 * P], mybir.AxisListType.X, ALU.max))
                step(V.tensor_scalar(col(20), col(20), 1e-30, None, ALU.max))
                step(V.reciprocal(col(21), col(20)))

            def power_of_two(dst, src):
                return V.tensor_scalar(dst.bitcast(i32), src.bitcast(i32), 0x7F800000, None, ALU.bitwise_and)

            def split3(dst, src, done):
                step(V.tensor_copy(dst[0:1, :], src[0:1, :]))
                step(V.tensor_copy(spare_bf, src))
                step(V.tensor_tensor(spare, src, spare_bf, ALU.subtract))
                step(V.tensor_copy(dst[32:33, :], spare[32:33, :]))
                step(V.tensor_copy(spare_bf, spare))
                step(V.tensor_tensor(spare, spare, spare_bf, ALU.subtract))
                done(V.tensor_copy(dst[64:65, :], spare[64:65, :]))

            step(V.memset(BROW[:, :], 0.0))
            step(V.memset(S1[:, :], 0.0))
            step(V.memset(S2, 0.0))
            step(V.memset(parts3[96:P, :], 1.0))

            def record(t4):
                for g in range(LG * LOAD_SLOTS):
                    n = t4 * (LG * LOAD_SLOTS) + g
                    dve.wait_ge(xt_ready, n + 1)
                    V.bn_stats(REC[:, ds(n * 6, 6)], XT[:, ds(n * GR, GR), :].rearrange("p r n -> p (r n)")
                               ).then_inc(bn_done, 1)

            with dve.Fori(0, ROWS // LOAD_ROWS // LOAD_SLOTS) as t4:
                record(t4)
            dve.wait_ge(bn_done, NG)
            group_norm(1)
            dve.wait_ge(consts_in, 16 * N_CONSTS)
            V.tensor_scalar(cs, NCF[:, L_CM:L_CM + P], col(6), None, ALU.mult).then_inc(small_in, 1)
            answer()
            step(V.tensor_copy(col(14), PS[:, 7, 4:5]))
            final(V.scalar_tensor_tensor(col(15), col(14), CF[:, C_NE0:C_NE0 + 1], CF[:, C_E0:C_E0 + 1],
                                         ALU.mult, ALU.add), norm_ready, 1)
            step(V.tensor_scalar(wW[:, 0:W_Z], RAW[:, 0:W_Z], VEC[:, V_LNW:V_LNW + 1], None, ALU.mult))
            step(V.tensor_scalar(wW[:, W_Z:W_N], RAW[:, W_Z:W_N], VEC[:, V_OW:V_OW + 1], None, ALU.mult))
            step(V.tensor_scalar(lnb_col, NCF[:, L_ECOL:L_ECOL + P], VEC[:, V_LNB:V_LNB + 1], None, ALU.mult))
            V.tensor_scalar(lnb_all, ones, VEC[:, V_OB:V_OB + 1], None, ALU.mult).then_inc(small_in, 1)
            answer()
            w_all = wW[:, 0:W_Z]
            step(V.tensor_copy(wW[:, 0:BANK], PS[:, 5, :]))
            step(V.tensor_copy(wW[:, W_G:W_Z], PS[:, 6, 0:P]))
            step(V.tensor_copy(EFF[:, W_Z:W_N], PS[:, 6, P:2 * P]))
            step(V.tensor_tensor(out_sq, EFF[:, W_Z:W_N], EFF[:, W_Z:W_N], ALU.mult))
            largest_weight()
            step(V.tensor_scalar(col(22), col(20), 1.0 / (W_TOP * Z_SCALE), None, ALU.mult))
            step(V.scalar_tensor_tensor(col(24), col(0), col(0), col(1), ALU.mult, ALU.add))
            step(V.tensor_scalar(col(24), col(24), float(ROWS * P), None, ALU.mult))
            step(V.scalar_tensor_tensor(col(24), PS[:, 7, 2 * P:2 * P + 1], float(CH), col(24), ALU.mult, ALU.add))
            step(V.tensor_copy(col(26), PS[:, 6, 3 * P:3 * P + 1]))
            step(V.scalar_tensor_tensor(col(24), col(26), col(26), col(24), ALU.mult, ALU.add))
            V.tensor_scalar(col(24), col(24), 3.0, 1e-20, ALU.mult, ALU.add).then_inc(bound_ready, 1)
            step(V.tensor_scalar(MS[:, 0:BANK], MS[:, 0:BANK], col(22), None, ALU.mult))
            step(V.tensor_scalar(w_all, w_all, col(21), W_TOP, ALU.mult, ALU.mult))
            step(V.tensor_copy(w_hi, w_all))
            step(V.tensor_tensor(w_lo, w_all, w_hi, ALU.subtract))
            split3(BROW[:, :], PS[:, 6, 2 * P:3 * P], lambda ins: final(ins, folded, 1))

            def normalise(t, last=False):
                dve.wait_ge(mm2_done, t * TG + TG)
                V.tensor_scalar(ve[0:96, :], PS[0:96, 4, :], EPS, None, ALU.add).then_inc(var_ready, 1)
                dve.wait_ge(std_ready, t + 2)
                r, w = rt[0:96, :], tmp[0:96, :]
                chain(t, V.reciprocal(r, sd[0:96, :]))
                chain(t, V.scalar_tensor_tensor(w, r, -0.5, r, ALU.mult, ALU.mult))
                chain(t, V.tensor_tensor(w, w, ve[0:96, :], ALU.mult))
                chain(t, V.scalar_tensor_tensor(r, w, 1.5, r, ALU.add, ALU.mult))
                reached(dve, bc_done, t * TG)
                chain(t, V.tensor_copy(parts3[0:96, :], r))
                chain(t, V.tensor_tensor(r, r, parts3[0:96, :], ALU.subtract))
                chain(t, V.tensor_copy(parts3[32:64, :], r[32:64, :]))
                chain(t, V.tensor_copy(parts3[64:96, :], r[64:96, :]))
                chain(t, V.tensor_tensor(r[64:96, :], r[64:96, :], parts3[64:96, :], ALU.subtract))
                V.tensor_copy(parts3[64:96, :], r[64:96, :]).then_inc(rb_ready, 1)
                for u in range(TG):
                    n = t * TG + u
                    dve.wait_ge(bc_done, n + 1)
                    if last and u >= 8:
                        if u - 8 in LOWS_V:
                            dve.wait_ge(lo_done_v, LOWS_V.index(u - 8) + 1)
                        else:
                            dve.wait_ge(lo_done, low_count(u - 8))
                    else:
                        reached(dve, lo_done, n - 7)
                    V.tensor_tensor(zn[:, u % 8], XT[:, ds(n * GR, GR), :].rearrange("p r n -> p (r n)"),
                                    PS[:, 5 + u % 2, :], ALU.mult).then_inc(zn_done, 1)
                    if not last:
                        if u > 0:
                            high(n - 1, (u - 1) % 8)
                    elif u - 2 in LOWS_V:
                        low(u - 2)
                if not last:
                    high(t * TG + TG - 1, (TG - 1) % 8)
                else:
                    assert LOWS_V[-1] < TG - 2

            def low(u):
                n = NG - TG + u
                dve.wait_ge(hi_done, n + 1)
                V.tensor_tensor(half(n, 1), zn[:, u % 8], half(n, 0), ALU.subtract).then_inc(lo_done_v, 1)

            def high(n, slot):
                dve.wait_ge(zn_done, n + 1)
                V.tensor_copy(half(n, 0), zn[:, slot]).then_inc(hi_done, 1)

            CHAIN = 9
            made = [0]

            def chain(t, ins):
                made[0] += 1
                ins.then_inc(dve_chain, 1)
                dve.wait_ge(dve_chain, t * CHAIN + made[0])

            def normalise_round(t, last=False):
                made[0] = 0
                normalise(t, last)
                assert made[0] == CHAIN

            normalise_round(0)
            dve.wait_ge(bound_root, 1)
            step(V.tensor_scalar(col(26), col(23), 1.0 / X_TOP, None, ALU.mult))
            step(power_of_two(col(24), col(26)))
            step(V.tensor_scalar(col(24), col(24), 2.0, None, ALU.mult))
            step(V.reciprocal(col(26), col(24)))
            step(V.tensor_scalar(col(26), col(26), 1.25, None, ALU.mult))
            step(power_of_two(col(25), col(26)))
            step(V.tensor_scalar(unscale[:, :], ident, col(24), None, ALU.mult))
            rounds(dve, normalise_round, NT, 1, lambda t: normalise_round(t, last=True), done=1)

            for layer in range(2):
                def products(q, g8):
                    for u in range(8):
                        n = q * NG + (g8 * 8 + u)
                        dve.wait_ge(msk_done, n + 1)
                        v = PS[:, u, :].rearrange("p (r q k) -> p q k r", q=2, k=4 * CHUNK)
                        w = sig[:, u % 4].rearrange("p (r q) k -> p q k r", q=2)
                        V.tensor_tensor(ab[:, :, :, ds(g8 * (8 * GR) + u * GR, GR)], v[:, :, 2 * CHUNK:4 * CHUNK, :],
                                        w, ALU.mult).then_inc(prod_done[0], 1)

                def add_biases(q, g0, us):
                    for u in us:
                        n = q * NG + (g0 + u)
                        dve.wait_ge(proj_done[1], n + 1)
                        reached(dve, prod_done[1], n - 3)
                        bias = bias_all[:, ds(q * QW, QW)].unsqueeze(1).to_broadcast([P, GR, QW])
                        V.scalar_tensor_tensor(biased[u % 4].rearrange("p (r m) -> p r m", m=QW),
                                               PS[:, u, :].rearrange("p (r m) -> p r m", m=QW), col(28), bias,
                                               ALU.mult, ALU.add).then_inc(bias_added, 1)

                def chunk(q, last=False):
                    if layer == 0:
                        with dve.Fori(0, NG // 8) as g8:
                            products(q, g8)
                    else:
                        add_biases(q, 0, range(AHEAD, 8))
                        with dve.Fori(1, NG // 8) as g8:
                            add_biases(q, g8 * 8, range(8))
                        if not last:
                            add_biases(q + 1, 0, range(AHEAD))
                    for c in range(CHUNK):
                        s = (c // 2) % 2
                        dve.wait_ge(st_ready, q * CHUNK + (c + 1 + CH * layer))
                        if layer == 0:
                            reached(dve, acc_done, q * CHUNK + c)
                            V.tensor_tensor(S1[:, :], S1[:, :], st[:, s, :, c % 2], ALU.add).then_inc(s1_done, 1)
                            dve.wait_ge(sqp_ready, q * CHUNK + (c + 1))
                            dve.wait_ge(s1_done, q * CHUNK + (c + 1))
                            V.tensor_tensor(S2, S2, sqp, ALU.add).then_inc(acc_done, 1)
                        else:
                            V.bn_stats(REC[:, ds((q * CHUNK + c) * 6, 6)], st[:, s, :, c % 2]).then_inc(acc_done, 1)

                if layer == 0:
                    dve.wait_ge(lo_done, low_count(TG - 1))
                    dve.wait_ge(lo_done_v, len(LOWS_V))
                    rounds(dve, chunk, NQ, 1)
                else:
                    add_biases(0, 0, range(AHEAD))
                    split3(BROW[:, :], EFF[:, W_Z:W_N], step)
                    rounds(dve, chunk, NQ, 0, lambda q: chunk(q, last=True))
                dve.wait_ge(acc_done, CH * (layer + 1))
                if layer == 0:
                    var = sqp
                    step(V.scalar_tensor_tensor(S1[:, :], S1[:, :], 1.0 / CH ** 2, S1[:, :], ALU.mult, ALU.mult))
                    step(V.scalar_tensor_tensor(var, S2, 1.0 / CH, S1[:, :], ALU.mult, ALU.subtract))
                    V.tensor_scalar(var, var, 0.0, EPS, ALU.max, ALU.add).then_inc(var_ready, 1)
                    dve.wait_ge(std_ready, NT + 2)

                    def rstd_rows(i):
                        def rows(tile):
                            return tile.rearrange("p (q r) -> p q r", q=2)[:, :, i * ROWS // 4:(i + 1) * ROWS // 4]

                        r, w = rows(S1[:, :]), rows_tmp[:, :].rearrange("p (q r) -> p q r", q=2)
                        step(V.reciprocal(r, r))
                        step(V.scalar_tensor_tensor(w, r, -0.5, r, ALU.mult, ALU.mult))
                        step(V.tensor_tensor(w, w, rows(var), ALU.mult))
                        return V.scalar_tensor_tensor(r, w, 1.5, r, ALU.add, ALU.mult)

                    final(rstd_rows(0), weights_ready, 1)
                else:
                    V.bn_aggr(T[:, 0:2], REC[:, :]).then_inc(small_in, 1)
                    answer()
                    step(V.tensor_scalar(col(2), PS[:, 7, 0:1], 1.0 / P, None, ALU.mult))
                    step(V.tensor_tensor(col(7), col(0), col(2), ALU.subtract))
                    V.scalar_tensor_tensor(col(3), col(7), col(7), col(1), ALU.mult, ALU.add).then_inc(small_in, 1)
                    answer()
                    V.tensor_scalar(col(4), PS[:, 7, 2:3], 1.0 / P, EPS, ALU.mult, ALU.add).then_inc(var_ready, 1)
                    step(rsqrt(col(6), col(4), col(5), NT + 5, col(7)))
                    step(V.tensor_tensor(col(6), col(6), VEC[:, V_AO:V_AO + 1], ALU.mult))
                    step(V.tensor_tensor(col(7), col(6), col(2), ALU.mult))
                    final(V.tensor_tensor(col(8), VEC[:, V_BO:V_BO + 1], col(7), ALU.subtract), weights_ready, 2)
                    for s in range(2):
                        dve.wait_ge(p_stored[s], 16 * (CH // 4) * 2)

                base = NG * layer

                def finish_steps(g0, n_steps, lo):
                    for k in range(n_steps):
                        g = g0 + k
                        if lo[0] <= k < lo[1]:
                            s, u = (k // BG) % 2, k % BG
                            if u == 0:
                                dve.wait_ge(p_in[s], g0 * 4 + 64 * (1 + NB // 2 * layer))
                            reached(dve, tb_done, g + (base - 1))
                            for q in range(1 + layer):
                                src = ptb[:, s].rearrange("p (c q) (r e) -> p q c r e", q=2, e=2)
                                dst = pn[:, k % 2].rearrange("p r (q c e) -> p q c r e", q=2, e=2)
                                tile = src[:, q, :, u * GR:(u + 1) * GR, :]
                                if layer == 0:
                                    rs = rstd2[:, q, ds(g * GR, GR)].unsqueeze(1).unsqueeze(3)
                                    ins = V.tensor_tensor(dst[:, q], tile, rs.to_broadcast([P, CH // 2, GR, 2]),
                                                          ALU.mult)
                                else:
                                    ins = V.tensor_copy(dst[:, q], tile)
                            ins.then_inc(pn_done, 1)
                            if layer == 0 and isinstance(g0, int) and g0 == 0 and k in (3, 6, 9):
                                final(rstd_rows(k // 3), rstd_ready, k // 3)
                        if layer == 1 and lo[4] <= k < lo[5]:
                            if isinstance(g, int) and g <= AHEAD:
                                gates = range(AHEAD) if g == 1 else ()
                            else:
                                gates = (g - 1,)
                            for h in gates:
                                ahead = isinstance(h, int) and h < AHEAD
                                place = h if ahead else (k - 1)
                                if ahead:
                                    dve.wait_ge(proj_done[1], NQ * NG + h + 1)
                                else:
                                    dve.wait_ge(g_done, h + (1 + NG - 2 * AHEAD))
                                    reached(dve, xadd_done, h + (base - 3))
                                bias = bias_all[:, W_G:W_Z].unsqueeze(1).to_broadcast([P, GR, ROW])
                                V.scalar_tensor_tensor(
                                    sg[place % 4].rearrange("p (r m) -> p r m", m=ROW),
                                    PS[:, h if ahead else place % 2, :].rearrange("p (r m) -> p r m", m=ROW),
                                    col(28), bias, ALU.mult, ALU.add).then_inc(gate_bias_added, 1)
                        if lo[2] <= k < lo[3]:
                            h = g - 2
                            dve.wait_ge(z_done, h + (1 + base))
                            dve.wait_ge(sg_done, h + (1 + base))
                            tile = sg[(k + 2) % 4]
                            V.tensor_tensor(tile, PS[:, 6 + k % 2, :], tile, ALU.mult).then_inc(y_done, 1)
                            if layer == 1:
                                if (k - 2) % HG == 0:
                                    reached(dve, xb_stored[(k - 2) // HG % HS], g - 2 - (k - 2) % 16)
                                dve.wait_ge(x1back_done, h + 1)
                                dve.wait_ge(y_done, h + (1 + base))
                                rows = xb[:, (k - 2) // HG % HS, (k - 2) % HG * GR:((k - 2) % HG + 1) * GR, :]
                                V.tensor_tensor(rows.rearrange("p r m -> p (r m)"), PS[:, 2 + k % 2, :], tile, ALU.add
                                                ).then_inc(xadd_done, 1)
                        if layer == 0:
                            split(k, g, lo)
                        if layer == 0 and lo[4] <= k < lo[5]:
                            h = g - 4
                            dve.wait_ge(x1tr_done, h + 1)
                            bank = new_x_bank(h) if isinstance(h, int) else 2 + k % 2
                            V.bn_stats(REC[:, ds(h * 6, 6)], PS[:, bank, :]).then_inc(bn_done, 1)

                def split(k, g, lo):
                    if lo[6] <= k < lo[7]:
                        h = g - 5
                        dve.wait_ge(x1t_ready, h + 1)
                        bank = new_x_bank(h) if isinstance(h, int) else 2 + (k + 1) % 2
                        V.scalar_tensor_tensor(half(h, 1), PS[:, bank, :], col(25), half(h, 0),
                                               ALU.mult, ALU.subtract).then_inc(x1split_done, 1)

                third = 4 if layer == 0 else 1
                finish_steps(0, 16, (0, 16, 2, 16, third, 16, 5, 16))
                with dve.Fori(1, NG // 16) as i:
                    finish_steps(i * 16, 16, (0, 16, 0, 16, 0, 16, 0, 16))
                finish_steps(NG, 5, (0, 0, 0, 2, 0, third, 0, 2))

                if layer == 0:
                    dve.wait_ge(bn_done, 2 * NG)
                    dve.wait_ge(raw1_in, 16)
                    group_norm(NT + 3, lambda: [split(k, NG + k, (0,) * 7 + (5,)) for k in range(2, 5)])
                    step(V.tensor_tensor(col(9), col(0), col(6), ALU.mult))
                    step(V.tensor_tensor(col(10), col(9), col(8), ALU.add))
                    step(V.tensor_tensor(col(11), col(6), col(6), ALU.mult))
                    step(V.tensor_tensor(col(11), col(11), col(1), ALU.mult))
                    V.scalar_tensor_tensor(col(11), col(10), col(10), col(11), ALU.mult, ALU.add).then_inc(small_in, 1)
                    answer()
                    step(V.tensor_scalar(T[:, 18:20], PS[:, 7, 4:6], 1.0 / P, None, ALU.mult))
                    step(V.scalar_tensor_tensor(col(7), col(18), col(18), col(19), ALU.mult, ALU.subtract))
                    V.tensor_scalar(col(16), col(7), -1.0, EPS, ALU.mult, ALU.add).then_inc(var_ready, 1)
                    step(rsqrt(col(13), col(16), col(17), NT + 4, col(7)))
                    step(V.tensor_tensor(col(13), col(13), VEC[:, V_AI:V_AI + 1], ALU.mult))
                    step(V.tensor_tensor(col(6), col(6), col(13), ALU.mult))
                    step(V.tensor_tensor(col(8), col(8), col(18), ALU.subtract))
                    step(V.scalar_tensor_tensor(col(8), col(8), col(13), VEC[:, V_BI:V_BI + 1], ALU.mult, ALU.add))
                    step(V.tensor_tensor(col(27), col(6), col(24), ALU.mult))
                    step(V.tensor_scalar(w_all, RAW[:, 0:W_Z], col(27), None, ALU.mult))
                    largest_weight(lambda: V.tensor_scalar(shift_all, ones, col(8), None, ALU.mult).then_inc(small_in, 1))
                    step(V.tensor_scalar(w_all, w_all, col(21), W_TOP, ALU.mult, ALU.mult))
                    step(V.tensor_copy(w_hi, w_all))
                    final(V.tensor_tensor(w_lo, w_all, w_hi, ALU.subtract), folded, 2)
                    step(V.tensor_scalar(col(28), col(20), 1.0 / W_TOP, None, ALU.mult))
                    answer()
                    step(V.tensor_copy(bias_all[:, 0:BANK], PS[:, 5, :]))
                    step(V.tensor_copy(bias_all[:, W_G:W_Z], PS[:, 6, 0:P]))
                    final(V.tensor_copy(EFF[:, W_Z:W_N], PS[:, 6, P:2 * P]), biases_ready, 1)

    return nc


def shape_constants():
    k = np.arange(P)
    par, c = k // CH, k % CH
    same = (par[:, None] == par[None, :])
    eye = np.eye(P)
    consts = np.zeros((P, C_N))
    consts[:, C_ID:C_ID + P] = eye
    consts[:, C_GM:C_GM + P] = (c[:, None] // 2 == c[None, :] // 2) / 4
    consts[:, C_ONES:C_ONES + P] = 1
    consts[:, C_E0] = c == 0
    consts[:, C_NE0] = c != 0
    norm = np.zeros((P, L_N))
    norm[:, L_CM:L_CM + P] = eye - same / CH
    norm[:, L_DROP:L_DROP + P] = (eye - (same & (c[:, None] == 0))) * (c[None, :] != 0)
    for part in range(3):
        norm[k, L_SEL + 30 + 32 * part + par] = 1 / CH
    norm[k, L_ECOL + CH * par] = 1
    norm[0, L_BSEL] = 1
    norm[1, L_BSEL + CH] = 1
    spread = np.zeros((P, TG, P))
    for part in range(3):
        for u in range(TG):
            for q in range(2):
                spread[32 * part + 2 * u + q, u, (par == q) & (c != 0)] = Z_SCALE
    spread[96, :, c == 0] = Z_SCALE
    ones3 = np.zeros((P, P))
    ones3[[0, 32, 64]] = 1
    return consts, norm, spread.reshape(P, TG * P), ones3


def kernel(**inputs):
    import concourse.bacc as bacc
    from concourse.bass_utils import run_bass_kernel_spmd as run
    import ml_dtypes

    a = {k: np.asarray(v) for k, v in inputs.items()}

    def weights(gate_a, gate_b, lin_a, lin_b, gate_o, lin_o):
        four = np.stack([gate_a, gate_b, lin_a, lin_b], 1).reshape(CH, 2, 2, NQ, CHUNK)
        four = four.transpose(0, 3, 1, 4, 2).reshape(CH, NQ, CH)
        cols = np.concatenate([four, gate_o[:, None], lin_o[:, None]], 1)
        gap = np.zeros_like(cols)
        even = np.stack([cols, gap], 2).reshape(CH, W_N)
        odd = np.stack([gap, cols], 2).reshape(CH, W_N)
        return np.ascontiguousarray(np.concatenate([even, odd], 0))

    def biases(gate_a, gate_b, lin_a, lin_b, gate_o, lin_o):
        four = np.stack([gate_a, gate_b, lin_a, lin_b], 0).reshape(2, 2, NQ, CHUNK)
        cols = np.concatenate([four.transpose(2, 0, 3, 1).reshape(NQ, CH), gate_o[None], lin_o[None]], 0)
        gap = np.zeros_like(cols)
        return np.stack([np.stack([cols, gap], 1).reshape(W_N), np.stack([gap, cols], 1).reshape(W_N)], 0)

    L0, L1 = "L0_conv_", "L1_conv_"
    names0 = [L0 + n for n in ("w_ag", "w_bg", "w_ap", "w_bp", "w_g", "w_z")]
    names1 = [L1 + n for n in ("W_ga", "W_gb", "W_la", "W_lb", "W_go", "W_lo")]
    bias0 = [L0 + n for n in ("b_ag", "b_bg", "b_ap", "b_bp", "b_g", "b_z")]
    bias1 = [L1 + n for n in ("b_ga", "b_gb", "b_la", "b_lb", "b_go", "b_lo")]
    vecs = [np.concatenate([a[L0 + n]] * 2) for n in ("ln_in_w", "ln_in_b", "ln_out_w", "ln_out_b")]
    vecs += [np.repeat(a[L1 + n], P) for n in ("alpha_in", "beta_in", "alpha_o", "beta_o")]
    consts, norm, spread, ones3 = shape_constants()
    arrays = {
        "x": np.ascontiguousarray(a["x"]),
        "mask": np.ascontiguousarray(a[L0 + "mask"]),
        "w0": weights(*(a[n] for n in names0)),
        "w1": weights(*(a[n].T for n in names1)),
        "bias0": biases(*(a[n] for n in bias0)),
        "bias1": biases(*(a[n] for n in bias1)),
        "vecs": np.ascontiguousarray(np.stack(vecs, 1)),
        "consts": consts.astype(np.float32),
        "norm_consts": norm.astype(np.float32),
        "spread": spread.astype(ml_dtypes.bfloat16),
        "ones3": ones3.astype(ml_dtypes.bfloat16),
    }
    nc = bacc.Bacc("TRN2", target_bir_lowering=False, num_devices=1, dynamic_dma_scratch_size=64)
    args = [nc.dram_tensor(n, v.shape, mybir.dt.from_np(v.dtype), kind="ExternalInput").ap()
            for n, v in arrays.items()]
    out = nc.dram_tensor("out", (1, ROWS, COLS, CH), mybir.dt.float32, kind="ExternalOutput").ap()
    build(nc, *args, out)
    r = run(nc, [arrays], core_ids=[0])
    return r.results[0]["out"]
```
